# Optimizing a Trainium2 kernel written in Bass

```python
import numpy as np
import jax
import jax.numpy as jnp

def _softmax(x, axis=-1):
    return jax.nn.softmax(x, axis=axis)
def _gelu(x):
    return jax.nn.gelu(x, approximate=True)
def _silu(x):
    return jax.nn.silu(x)
def _sigmoid(x):
    return jax.nn.sigmoid(x)
def _layernorm(x, axis=-1, eps=1e-5):
    m = jnp.mean(x, axis=axis, keepdims=True)
    v = jnp.var(x, axis=axis, keepdims=True)
    return (x - m) / jnp.sqrt(v + eps)
def _scatter_add(tgt, idx, src, axis=0):
    return tgt.at[idx].add(src)
def _segment_sum(src, seg, n):
    return jax.ops.segment_sum(src, seg, n)

kernel_name = 'mk_adj_resnorm_d1_adj_512_bc9177'

def setup_inputs(seed: int = 0):
    np.random.seed(seed)
    _w = jnp.asarray
    def _rec_inputs():
        import jax
        import jax.numpy as jnp
        _gk = jax.random.key(seed)
        x = 7.22e-05 + 1 * jax.random.normal(jax.random.fold_in(_gk, 1), (16, 1024, 512), jnp.float32)
        _w = (1.0 + jnp.arange(1024, dtype=jnp.float32)) ** -0.5
        _w = _w / _w.mean()
        _pij = jnp.clip(0.00390625 * _w[:, None] * _w[None, :], 0.0, 1.0)
        _a = jax.random.uniform(jax.random.fold_in(_gk, 2), (16, 1024, 1024)) < _pij
        adj = _a.astype(jnp.int32)
        return x, adj
    x, adj = _rec_inputs()
    def _L0_gnn_setup():
        import jax, jax.numpy as jnp
        import numpy as np
        EMBED_DIM = 512
        N_HEADS = 8
        HEAD_DIM = EMBED_DIM // N_HEADS
        NEG_INF = -1000000000.0
        key = jax.random.key(seed)
        ks = jax.random.split(key, 10)
        bs, n_agents = (64, 256)
        inputs = jax.random.normal(ks[0], (bs, n_agents, EMBED_DIM), dtype=jnp.float32)
        adj = jax.random.randint(ks[1], (bs, n_agents, n_agents), 0, 2, dtype=jnp.int32)
        s = 1.0 / np.sqrt(EMBED_DIM)
        Wq = jax.random.normal(ks[2], (EMBED_DIM, EMBED_DIM), dtype=jnp.float32) * s
        Wk = jax.random.normal(ks[3], (EMBED_DIM, EMBED_DIM), dtype=jnp.float32) * s
        Wv = jax.random.normal(ks[4], (EMBED_DIM, EMBED_DIM), dtype=jnp.float32) * s
        Wo = jax.random.normal(ks[5], (EMBED_DIM, EMBED_DIM), dtype=jnp.float32) * s
        bq = jnp.zeros((EMBED_DIM,), jnp.float32)
        bk = jnp.zeros((EMBED_DIM,), jnp.float32)
        bv = jnp.zeros((EMBED_DIM,), jnp.float32)
        bo = jnp.zeros((EMBED_DIM,), jnp.float32)
        return {'inputs': inputs, 'adj': adj, 'Wq': Wq, 'bq': bq, 'Wk': Wk, 'bk': bk, 'Wv': Wv, 'bv': bv, 'Wo': Wo, 'bo': bo}
    _L0_gnn_all = _L0_gnn_setup()
    _L0_gnn_in = {k: v for k, v in _L0_gnn_all.items() if k in ('Wq', 'bq', 'Wk', 'bk', 'Wv', 'bv', 'Wo', 'bo', )}
    del _L0_gnn_all

    return {
        "x": x,
        "adj": adj,
        "L0_gnn_Wq": _L0_gnn_in["Wq"],
        "L0_gnn_bq": _L0_gnn_in["bq"],
        "L0_gnn_Wk": _L0_gnn_in["Wk"],
        "L0_gnn_bk": _L0_gnn_in["bk"],
        "L0_gnn_Wv": _L0_gnn_in["Wv"],
        "L0_gnn_bv": _L0_gnn_in["bv"],
        "L0_gnn_Wo": _L0_gnn_in["Wo"],
        "L0_gnn_bo": _L0_gnn_in["bo"],
    }

def reference(x, adj, L0_gnn_Wq, L0_gnn_bq, L0_gnn_Wk, L0_gnn_bk, L0_gnn_Wv, L0_gnn_bv, L0_gnn_Wo, L0_gnn_bo):
    import jax
    import jax.numpy as jnp
    def _L0_gnn_ref(inputs, adj, Wq, bq, Wk, bk, Wv, bv, Wo, bo):
        import jax, jax.numpy as jnp
        import numpy as np
        EMBED_DIM = 512
        N_HEADS = 8
        HEAD_DIM = EMBED_DIM // N_HEADS
        NEG_INF = -1000000000.0
        bs, n, _ = inputs.shape
        q = (inputs @ Wq + bq).reshape(bs, n, N_HEADS, HEAD_DIM)
        k = (inputs @ Wk + bk).reshape(bs, n, N_HEADS, HEAD_DIM)
        v = (inputs @ Wv + bv).reshape(bs, n, N_HEADS, HEAD_DIM)
        logits = jnp.einsum('bqhd,bkhd->bhqk', q, k) / np.sqrt(HEAD_DIM)
        mask = (adj > 0)[:, None, :, :]
        logits = jnp.where(mask, logits, NEG_INF)
        attn = jax.nn.softmax(logits, axis=-1)
        out = jnp.einsum('bhqk,bkhd->bqhd', attn, v).reshape(bs, n, EMBED_DIM)
        out = out @ Wo + bo
        return jax.nn.relu(out)

    x = _layernorm(x + _L0_gnn_ref(x, adj, L0_gnn_Wq, L0_gnn_bq, L0_gnn_Wk, L0_gnn_bk, L0_gnn_Wv, L0_gnn_bv, L0_gnn_Wo, L0_gnn_bo), axis=-1)
    return x


_drawn_inputs = setup_inputs


def setup_inputs(seed=0):
    import zlib

    import numpy as np

    out = dict(_drawn_inputs(seed))
    spreads = {'L0_gnn_bq': (0.0, 0.348),
     'L0_gnn_bk': (0.0, 0.8),
     'L0_gnn_bv': (0.0, 0.1),
     'L0_gnn_bo': (0.0, 0.1)}
    factors = {}
    for name, (base, spread) in spreads.items():
        noise = np.random.default_rng([zlib.crc32(name.encode()), seed]).standard_normal(out[name].shape)
        drawn = base * np.exp(spread * noise) if base else spread * noise
        out[name] = jnp.asarray(drawn.astype(out[name].dtype))
    for name, factor in factors.items():
        out[name] = (out[name] * factor).astype(out[name].dtype)
    return out
```

```python
import concourse.bass as bass
from concourse import mybir
from contextlib import ExitStack

F32 = mybir.dt.float32
F32R = mybir.dt.float32r
BF16 = mybir.dt.bfloat16
I32 = mybir.dt.int32
ALU = mybir.AluOpType
ACT = mybir.ActivationFunctionType

P = 128
BATCH, N, D = 16, 1024, 512
HEADS = 8
HD = D // HEADS
PAIRS = HEADS // 2
KD = D // P
QT = N // P
HALF = 512
SCALE = HD ** -0.5
MASKED = -1e30
LN_EPS = 1e-5


def project(nc, x, wq, bq, wk, bk, wv, bv, qk_parts, v_all):
    XT_ITEMS, QK_ITEMS, V_ITEMS = QT, 2 * PAIRS * 2, QT
    ITEMS = XT_ITEMS + QK_ITEMS + V_ITEMS
    SPLITS = XT_ITEMS + QK_ITEMS
    BANKS = 8

    with ExitStack() as ctx:
        def sb(name, shape, dt):
            return ctx.enter_context(nc.sbuf_tensor(name, shape, dt))

        def sem(name):
            return ctx.enter_context(nc.semaphore(name))

        w_raw = sb("w_raw", [P, 3, KD, D], F32)
        w_hi = sb("w_hi", [P, 3, KD, D], F32R)
        w_lo = sb("w_lo", [P, 3, KD, D], F32R)
        bias_qk = sb("bias_qk", [P, 2, PAIRS], F32)
        bias_v = sb("bias_v", [P, D], F32)
        ident = sb("ident", [P, P], F32)
        x_in = sb("x_in", [P, QT, D], F32)
        xt_hi = sb("xt_hi", [P, KD, N], F32R)
        xt_lo = sb("xt_lo", [P, KD, N], F32R)
        out_hi = sb("out_hi", [P, 2, N], F32R)
        out_lo = sb("out_lo", [P, 2, N], F32R)
        out_v = sb("out_v", [P, 2, D], F32)
        bank = [ctx.enter_context(nc.psum_tensor(f"bank{n}", [P, HALF], F32)) for n in range(BANKS)]

        w_in = sem("w_in")
        w_hi_done = sem("w_hi_done")
        w_lo_done = sem("w_lo_done")
        ident_zero = sem("ident_zero")
        ident_done = sem("ident_done")
        x_loaded = sem("x_loaded")
        filled = sem("filled")
        hi_done = sem("hi_done")
        emptied = sem("emptied")
        qk_free = [sem(f"qk_free{n}") for n in range(2)]
        v_free = [sem(f"v_free{n}") for n in range(2)]

        block = ctx.enter_context(nc.Block())

        @block.gpsimd
        def _(pool):
            nc.gpsimd.memset(ident[:, :], 0.0).then_inc(ident_zero, 1)
            pool.wait_ge(ident_zero, 1)
            nc.gpsimd.affine_select(out=ident[:, :], in_=ident[:, :], compare_op=ALU.not_equal, fill=1.0,
                                    base=0, pattern=[[-1, P]], channel_multiplier=1).then_inc(ident_done, 1)
            pool.dma_start(x_in[:, :, :], x[0, :, :].rearrange("(t p) d -> p t d", p=P)).then_inc(x_loaded, 16)
            with pool.Fori(1, BATCH) as b:
                pool.wait_ge(filled, b * ITEMS - (ITEMS - XT_ITEMS))
                pool.dma_start(x_in[:, :, :],
                               x[bass.ds(b, 1), :, :].rearrange("o (t p) d -> p (o t) d", p=P)).then_inc(x_loaded, 16)

        @block.sync
        def _(sp):
            for n, w in enumerate((wq, wk, wv)):
                sp.dma_start(w_raw[:, n, :, :], w.rearrange("(k p) n -> p k n", p=P)).then_inc(w_in, 16)
            with nc.allow_non_contiguous_dma(reason="512 bias values, once"):
                for n, v in enumerate((bq, bk)):
                    sp.dma_start(bias_qk[:, n, :], v.rearrange("(g p) -> p g", p=P)).then_inc(w_in, 16)
            sp.dma_start(bias_v[:, :], bv.rearrange("(a n) -> a n", a=1).to_broadcast([P, D])).then_inc(w_in, 16)
            with sp.Fori(0, BATCH) as b:
                for g in range(2 * PAIRS):
                    which, pair = g // PAIRS, g % PAIRS
                    sp.wait_ge(emptied, b * ITEMS + (XT_ITEMS + 2 * g + 2))
                    for part, src in enumerate((out_hi, out_lo)):
                        sp.dma_start(qk_parts[bass.ds(b, 1), 2 * which + part, pair * P:(pair + 1) * P, :]
                                     .rearrange("o p n -> p (o n)").bitcast(F32),
                                     src[:, g % 2, :].bitcast(F32)).then_inc(qk_free[g % 2], 16)
                for t in range(V_ITEMS):
                    sp.wait_ge(emptied, b * ITEMS + (SPLITS + t + 1))
                    sp.dma_start(v_all[bass.ds(b, 1), t * P:(t + 1) * P, :].rearrange("o p n -> p (o n)"),
                                 out_v[:, t % 2, :]).then_inc(v_free[t % 2], 16)
            for n in range(2):
                sp.wait_ge(qk_free[n], 32 + BATCH * PAIRS * 32)
                sp.wait_ge(v_free[n], 16 + BATCH * V_ITEMS // 2 * 16)

        @block.tensor
        def _(pe):
            pe.wait_ge(ident_done, 1)
            pe.wait_ge(w_hi_done, 3)
            pe.wait_ge(w_lo_done, 3)

            def product(out, parts):
                terms = [(a, b, k) for a, b in ((0, 0), (0, 1), (1, 0)) for k in range(KD)]
                for n, (a, b, k) in enumerate(terms):
                    lhs, rhs = parts(a, b, k)
                    last = nc.tensor.matmul(out, lhs, rhs, start=n == 0, stop=n == len(terms) - 1)
                last.then_inc(filled, 1)

            xt, w = (xt_hi, xt_lo), (w_hi, w_lo)
            with pe.Fori(0, BATCH) as b:
                pe.wait_ge(x_loaded, b * 16 + 16)
                for t in range(XT_ITEMS):
                    for k in range(KD):
                        last = nc.tensor.transpose(bank[t][:, k * P:(k + 1) * P], x_in[:, t, k * P:(k + 1) * P],
                                                   ident[:, :])
                    last.then_inc(filled, 1)
                for n in range(QK_ITEMS):
                    item = XT_ITEMS + n
                    which, pair, half = n // (2 * PAIRS), n // 2 % PAIRS, n % 2
                    pe.wait_ge(emptied, b * ITEMS + max(item - BANKS + 1, (half + 1) * XT_ITEMS // 2))
                    product(bank[item % BANKS][:, :],
                            lambda i, j, k: (w[i][:, which, k, pair * P:(pair + 1) * P],
                                             xt[j][:, k, half * HALF:(half + 1) * HALF]))
                for t in range(V_ITEMS):
                    item = SPLITS + t
                    pe.wait_ge(emptied, b * ITEMS + (item - BANKS + 1))
                    product(bank[item % BANKS][:, :],
                            lambda i, j, k: (xt[i][:, k, t * P:(t + 1) * P], w[j][:, 2, k, :]))
                pe.wait_ge(emptied, b * ITEMS + ITEMS)
                pe.nop(nofuse=True)

        @block.scalar
        def _(act):
            for n in range(3):
                act.wait_ge(w_in, 6 * 16)
                nc.scalar.activation(w_hi[:, n, :, :], w_raw[:, n, :, :], ACT.Copy).then_inc(w_hi_done, 1)
            for n in range(2):
                act.nop().then_inc(qk_free[n], 32)
            with act.Fori(0, BATCH) as b:
                for t in range(XT_ITEMS):
                    act.wait_ge(filled, b * ITEMS + (t + 1))
                    nc.scalar.activation(xt_hi[:, :, t * P:(t + 1) * P],
                                         bank[t][:, :].rearrange("p (k n) -> p k n", k=KD),
                                         ACT.Copy).then_inc(hi_done, 1)
                for n in range(QK_ITEMS):
                    item = XT_ITEMS + n
                    g, half = n // 2, n % 2
                    which, pair = g // PAIRS, g % PAIRS
                    if half == 0:
                        act.wait_ge(qk_free[g % 2], b * (PAIRS * 32) + (g // 2 + 1) * 32)
                    act.wait_ge(filled, b * ITEMS + (item + 1))
                    nc.scalar.activation(out_hi[:, g % 2, half * HALF:(half + 1) * HALF], bank[item % BANKS][:, :],
                                         ACT.Identity, bias=bias_qk[:, which, pair:pair + 1]).then_inc(hi_done, 1)

        @block.vector
        def _(dve):
            dve.wait_ge(w_in, 6 * 16)
            for n in range(3):
                dve.wait_ge(w_hi_done, n + 1)
                nc.vector.tensor_tensor(w_lo[:, n, :, :], w_raw[:, n, :, :], w_hi[:, n, :, :].bitcast(F32),
                                        ALU.subtract).then_inc(w_lo_done, 1)
            for n in range(2):
                dve.nop().then_inc(v_free[n], 16)
            with dve.Fori(0, BATCH) as b:
                for t in range(XT_ITEMS):
                    dve.wait_ge(hi_done, b * SPLITS + (t + 1))
                    nc.vector.tensor_tensor(xt_lo[:, :, t * P:(t + 1) * P],
                                            bank[t][:, :].rearrange("p (k n) -> p k n", k=KD),
                                            xt_hi[:, :, t * P:(t + 1) * P].bitcast(F32),
                                            ALU.subtract).then_inc(emptied, 1)
                for n in range(QK_ITEMS):
                    item = XT_ITEMS + n
                    g, half = n // 2, n % 2
                    which, pair = g // PAIRS, g % PAIRS
                    cols = slice(half * HALF, (half + 1) * HALF)
                    dve.wait_ge(hi_done, b * SPLITS + (item + 1))
                    nc.vector.scalar_tensor_tensor(out=out_lo[:, g % 2, cols], in0=bank[item % BANKS][:, :],
                                                   scalar=bias_qk[:, which, pair:pair + 1],
                                                   in1=out_hi[:, g % 2, cols].bitcast(F32),
                                                   op0=ALU.add, op1=ALU.subtract).then_inc(emptied, 1)
                for t in range(V_ITEMS):
                    item = SPLITS + t
                    dve.wait_ge(v_free[t % 2], b * (V_ITEMS // 2 * 16) + (t // 2 + 1) * 16)
                    dve.wait_ge(filled, b * ITEMS + (item + 1))
                    nc.vector.tensor_tensor(out_v[:, t % 2, :], bank[item % BANKS][:, :], bias_v[:, :],
                                            ALU.add).then_inc(emptied, 1)


def attend(nc, x, adj, wo, bo, qk_parts, v_all, out):
    ROUND = 2
    ROUNDS = BATCH // ROUND
    TILES = ROUND * HEADS * QT
    UNIT = 4
    UNITS = TILES // UNIT
    BT = HEADS * QT
    AHEAD = 3
    CH = UNIT // 2 * P
    O_ITEMS = ROUND * QT

    def head(t):
        return t // QT

    def o_slot(o):
        return o // QT * BT + (BT - 3 if o % QT < 4 else BT - 2) + o % QT

    with ExitStack() as ctx:
        def sb(name, shape, dt):
            return ctx.enter_context(nc.sbuf_tensor(name, shape, dt))

        def pb(name, shape, dt):
            return ctx.enter_context(nc.psum_tensor(name, shape, dt))

        def sem(name):
            return ctx.enter_context(nc.semaphore(name))

        wo_hi = sb("wo_hi", [P, 2, PAIRS, D], F32R)
        wo_lo = sb("wo_lo", [P, 2, PAIRS, D], F32R)
        bias_o = sb("bias_o", [P, D], F32)
        ident = sb("ident2", [P, P], F32)
        q_stack = sb("q_stack", [P, 2, N], F32R)
        k_hi = sb("k_hi", [P, 2, N], F32R)
        k_lo = sb("k_lo", [P, 2, N], F32R)
        v_pair = sb("v_pair", [P, 2, QT, P], F32)
        adj_in = sb("adj_in", [P, 2, N], I32)
        mask = sb("mask", [P, ROUND, QT, N], BF16)
        prob = sb("prob", [P, 4, N], F32)
        wo_raw = prob[:, 0:2, :].rearrange("p a (g n) -> p (a g) n", g=2)
        neg_max = sb("neg_max", [P, 4], F32)
        row_sum = sb("row_sum", [P, 4], F32)
        row_inv = sb("row_inv", [P, 4], F32)
        prob_t = sb("prob_t", [P, 2, QT, 2, CH], F32)
        att_hi = sb("att_hi", [P, PAIRS, 2, 2, CH], F32R)
        att_lo = sb("att_lo", [P, PAIRS, 2, 2, CH], F32R)
        x_res = sb("x_res", [P, 2, D], F32)
        y = sb("y", [P, D], F32)
        z = sb("z", [P, 4, D], F32)
        stats = sb("stats", [P, 6], F32)
        mean_var = sb("mean_var", [P, 2, 2], F32)
        half_power = sb("half_power", [P, 1], F32)
        var_eps = sb("var_eps", [P, 1], F32)
        inv_std = sb("inv_std", [P, 1], F32)

        score = [pb(f"score{n}", [P, N], F32) for n in range(2)]
        turned = [pb(f"turned{n}", [P, HALF], F32) for n in range(2)]
        mixed = pb("mixed", [P, HALF], F32)
        outp = pb("outp", [P, HALF], F32)

        wo_in = sem("wo_in")
        wo_hi_done = sem("wo_hi_done")
        wo_lo_done = sem("wo_lo_done")
        ident_zero = sem("ident2_zero")
        ident_done = sem("ident2_done")
        head_in = [sem(f"head_in{n}") for n in range(2)]
        v_in = [sem(f"v_in{n}") for n in range(2)]
        adj_loaded = [sem(f"adj_loaded{n}") for n in range(2)]
        x_in = [sem(f"x_in{n}") for n in range(2)]
        masks_made = sem("masks_made")
        scored = sem("scored")
        masked = sem("masked")
        exped = sem("exped")
        inverted = sem("inverted")
        normed = sem("normed")
        transposed = sem("transposed")
        kept = [sem("kept_low"), sem("kept_high")]
        mixed_done = sem("mixed_done")
        att_hi_done = sem("att_hi_done")
        att_done = sem("att_done")
        projected = sem("projected")
        biased = sem("biased")
        summed = sem("summed")
        stat_done = sem("stat_done")
        ready = sem("ready")
        var_done = sem("var_done")
        std_done = sem("std_done")
        finished = sem("finished")
        z_free = [sem(f"z_free{n}") for n in range(4)]

        block = ctx.enter_context(nc.Block())

        def batch_rows(t, b, j, q):
            return t[bass.ds(b * ROUND + j, 1), q * P:(q + 1) * P, :].rearrange("o p n -> p (o n)")

        def load_heads(q, r):
            for h in range(ROUND * HEADS):
                j, hh, buf = h // HEADS, h % HEADS, h % 2
                if h >= 2:
                    q.wait_ge(scored, r * TILES + (h - 1) * QT)
                rows = slice(hh * HD, (hh + 1) * HD)
                for dst, parts in ((q_stack, (0, 1)), (k_hi, (2, 2)), (k_lo, (3, 3))):
                    for n, part in enumerate(parts):
                        q.dma_start(dst[n * HD:(n + 1) * HD, buf, :].bitcast(F32),
                                    qk_parts[bass.ds(r * ROUND + j, 1), part, rows, :]
                                    .rearrange("o p n -> p (o n)").bitcast(F32)).then_inc(head_in[buf], 16)
                if hh % 2 == 0:
                    pair = h // 2
                    if pair >= 2:
                        q.wait_ge(mixed_done, r * UNITS + (pair - 1) * 4)
                    q.dma_start(v_pair[:, pair % 2, :, :],
                                v_all[bass.ds(r * ROUND + j, 1), :, hh * HD:(hh + 2) * HD]
                                .rearrange("o (t p) d -> p (o t) d", p=P)).then_inc(v_in[pair % 2], 16)

        @block.sync
        def _(sp):
            for n in range(2):
                if n:
                    sp.wait_ge(wo_lo_done, n)
                for h in range(2):
                    sp.dma_start(wo_raw[h * HD:(h + 1) * HD, :, :],
                                 wo.rearrange("(g two p) n -> two p g n", two=2, p=HD)[(h + n) % 2, :, :, :]).then_inc(wo_in, 16)
            sp.dma_start(bias_o[:, :], bo.rearrange("(a n) -> a n", a=1).to_broadcast([P, D])).then_inc(wo_in, 16)
            with sp.Fori(0, ROUNDS) as r:
                load_heads(sp, r)
                sp.wait_ge(mixed_done, r * UNITS + UNITS)
                sp.nop(nofuse=True)

        @block.gpsimd
        def _(pool):
            nc.gpsimd.memset(ident[:, :], 0.0).then_inc(ident_zero, 1)
            pool.wait_ge(ident_zero, 1)
            nc.gpsimd.affine_select(out=ident[:, :], in_=ident[:, :], compare_op=ALU.not_equal, fill=1.0,
                                    base=0, pattern=[[-1, P]], channel_multiplier=1).then_inc(ident_done, 1)
            nc.gpsimd.memset(half_power[:, :], -0.5).then_inc(ident_done, 1)

            def make_mask(r, j, q):
                n = j * QT + q
                pool.wait_ge(adj_loaded[n % 2], r * (ROUND * QT // 2 * 16) + (n // 2 + 1) * 16)
                pool.nop(nofuse=True)
                nc.gpsimd.tensor_scalar(mask[:, j, q, :], adj_in[:, n % 2, :], 0.0, MASKED,
                                        ALU.is_le, ALU.mult).then_inc(masks_made, 1)

            def normalise(r, t):
                pool.wait_ge(inverted, r * TILES + (t + 1))
                pool.nop(nofuse=True)
                nc.gpsimd.tensor_scalar(prob[:, t % 4, :], prob[:, t % 4, :], row_inv[:, t % 4:t % 4 + 1], 1.0,
                                        ALU.mult, ALU.mult).then_inc(normed, 1)

            def finish(r, o):
                pool.wait_ge(ready, r * O_ITEMS + (o + 1))
                pool.nop(nofuse=True)
                nc.gpsimd.tensor_scalar(var_eps[:, :], mean_var[:, o % 2, 1:2], LN_EPS, None,
                                        ALU.add).then_inc(var_done, 1)
                pool.wait_ge(var_done, r * O_ITEMS + (o + 1))
                nc.gpsimd.tensor_tensor(inv_std[:, :], var_eps[:, :], half_power[:, :], ALU.pow).then_inc(std_done, 1)
                pool.wait_ge(std_done, r * O_ITEMS + (o + 1))
                pool.nop(nofuse=True)
                nc.gpsimd.tensor_scalar(z[:, o % 4, :], z[:, o % 4, :], mean_var[:, o % 2, 0:1], inv_std[:, :],
                                        ALU.subtract, ALU.mult).then_inc(finished, 1)

            pool.wait_ge(ident_done, 2)
            with pool.Fori(0, ROUNDS) as r:
                for q in range(4):
                    make_mask(r, 0, q)
                for t in range(-AHEAD, TILES + 9):
                    for o in range(O_ITEMS):
                        if o_slot(o) == t:
                            finish(r, o)
                    if t == TILES:
                        pool.wait_ge(masked, r * TILES + TILES)
                    if 0 <= t + AHEAD < TILES:
                        normalise(r, t + AHEAD)
                    if 4 <= t + AHEAD + 4 < QT:
                        make_mask(r, 0, t + AHEAD + 4)
                    if 16 <= t < 16 + 4 * QT and t % 4 == 0:
                        make_mask(r, 1, (t - 16) // 4)

        @block.tensor
        def _(pe):
            pe.wait_ge(ident_done, 2)
            pe.wait_ge(wo_lo_done, 2)

            def scores(r, t):
                h, q = head(t), t % QT
                buf = h % 2
                if q == 0:
                    pe.wait_ge(head_in[buf], r * (ROUND * HEADS // 2 * 96) + (h // 2 + 1) * 96)
                if t >= 2:
                    pe.wait_ge(masked, r * TILES + (t - 1))
                for n, k in enumerate((k_hi, k_lo)):
                    for half in range(2):
                        cols = slice(half * HALF, (half + 1) * HALF)
                        last = nc.tensor.matmul(score[t % 2][:, cols], q_stack[:, buf, q * P:(q + 1) * P],
                                                k[:, buf, cols], start=n == 0, stop=n == 1)
                last.then_inc(scored, 1)

            def turn(r, t):
                pe.wait_ge(normed, r * TILES + (t + 1))
                for half in range(2):
                    if t >= 1:
                        pe.wait_ge(kept[half], r * TILES + t)
                    for n in range(4):
                        k = half * 4 + n
                        last = nc.tensor.transpose(turned[half][:, n * P:(n + 1) * P],
                                                   prob[:, t % 4, k * P:(k + 1) * P], ident[:, :])
                    last.then_inc(transposed, 1)

            def mix(r, u):
                h = head(u * UNIT)
                pair = h // 2
                if u % 4 == 0:
                    pe.wait_ge(v_in[pair % 2], r * (ROUND * PAIRS // 2 * 16) + (pair // 2 + 1) * 16)
                for half in range(2):
                    pe.wait_ge(kept[half], r * TILES + (u + 1) * UNIT)
                if u >= 1:
                    pe.wait_ge(att_done, r * UNITS + u)
                for k in range(QT):
                    for n in range(2):
                        chunk = n if h % 2 == 0 else 1 - n
                        last = nc.tensor.matmul(mixed[n * HD:(n + 1) * HD, 0:CH],
                                                v_pair[:, pair % 2, k, h % 2 * HD:(h % 2 + 1) * HD],
                                                prob_t[:, u % 2, k, chunk, :], start=k == 0, stop=k == QT - 1)
                last.then_inc(mixed_done, 1)

            def project_out(r, o):
                q = o % QT
                unit_half, chunk, off = q // 4, q % 4 // 2, q % 2 * P
                last_unit = o // QT * (UNITS // ROUND) + UNITS // ROUND - 2 + unit_half
                pe.wait_ge(att_done, r * UNITS + (last_unit + 1))
                if o >= 1:
                    pe.wait_ge(biased, r * O_ITEMS + o)
                att, w = (att_hi, att_lo), (wo_hi, wo_lo)
                terms = [(a, c, g) for a, c in ((0, 0), (0, 1), (1, 0)) for g in range(PAIRS)]
                for n, (a, c, g) in enumerate(terms):
                    last = nc.tensor.matmul(outp[:, :], att[a][:, g, unit_half, chunk, off:off + P],
                                            w[c][:, chunk, g, :], start=n == 0, stop=n == len(terms) - 1)
                last.then_inc(projected, 1)

            with pe.Fori(0, ROUNDS) as r:
                for t in range(-AHEAD, TILES + 8):
                    if t + AHEAD < TILES:
                        scores(r, t + AHEAD)
                    if 0 <= t < TILES:
                        turn(r, t)
                    if t > 0 and t % UNIT == 0 and t <= TILES:
                        mix(r, t // UNIT - 1)
                    for o in range(O_ITEMS):
                        if o_slot(o) == t:
                            project_out(r, o)
                pe.wait_ge(masked, r * TILES + TILES)
                pe.wait_ge(kept[0], r * TILES + TILES)
                pe.wait_ge(kept[1], r * TILES + TILES)
                pe.wait_ge(att_done, r * UNITS + UNITS)
                pe.wait_ge(biased, r * O_ITEMS + O_ITEMS)
                pe.nop(nofuse=True)

        def turned_out(half, t):
            in_unit = t % UNIT
            off = in_unit % 2 * P
            return prob_t[:, t // UNIT % 2, half * 4:half * 4 + 4, in_unit // 2, off:off + P]

        def att_part(att, u, n):
            h = head(u * UNIT)
            chunk = n if h % 2 == 0 else 1 - n
            return att[n * HD:(n + 1) * HD, h % HEADS // 2, u % 2, chunk, :]

        @block.scalar
        def _(act):
            for n in range(2):
                act.wait_ge(wo_in, 32 if n == 0 else 80)
                nc.scalar.activation(wo_hi[:, n, :, :], wo_raw[:, :, :], ACT.Copy).then_inc(wo_hi_done, 1)

            def load_adj(r, n):
                if n >= 2:
                    act.wait_ge(masks_made, r * (ROUND * QT) + (n - 1))
                act.dma_start(adj_in[:, n % 2, :], batch_rows(adj, r, n // QT, n % QT)).then_inc(adj_loaded[n % 2], 16)

            def load_x(r, o):
                if o >= 2:
                    act.wait_ge(summed, r * O_ITEMS + (o - 1))
                act.dma_start(x_res[:, o % 2, :], batch_rows(x, r, o // QT, o % QT)).then_inc(x_in[o % 2], 16)

            def store(r, o):
                act.wait_ge(finished, r * O_ITEMS + (o + 1))
                act.dma_start(batch_rows(out, r, o // QT, o % QT), z[:, o % 4, :]).then_inc(z_free[o % 4], 16)

            def exponential(r, t):
                act.wait_ge(masked, r * TILES + (t + 1))
                nc.scalar.activation(prob[:, t % 4, :], prob[:, t % 4, :], ACT.Exp, bias=neg_max[:, t % 4:t % 4 + 1],
                                     scale=-1.0, accum_out=row_sum[:, t % 4:t % 4 + 1]).then_inc(exped, 1)

            def keep_low(r, t):
                act.wait_ge(transposed, r * (2 * TILES) + (2 * t + 1))
                if t % UNIT == 0:
                    if t // UNIT >= 2:
                        act.wait_ge(mixed_done, r * UNITS + (t // UNIT - 1))
                nc.scalar.activation(turned_out(0, t), turned[0][:, :].rearrange("p (k n) -> p k n", k=4),
                                     ACT.Copy).then_inc(kept[0], 1)

            def att_high(r, u):
                act.wait_ge(mixed_done, r * UNITS + (u + 1))
                if u // (UNITS // ROUND) and u % (UNITS // ROUND) < 2:
                    act.wait_ge(projected, r * O_ITEMS + ((u // (UNITS // ROUND) - 1) * QT + (u % 2 + 1) * 4))
                for n in range(2):
                    nc.scalar.activation(att_part(att_hi, u, n), mixed[n * HD:(n + 1) * HD, 0:CH],
                                         ACT.Copy).then_inc(att_hi_done, 1)

            with act.Fori(0, ROUNDS) as r:
                for n in range(2):
                    load_adj(r, n)
                    load_x(r, n)
                for t in range(-AHEAD, TILES + 10):
                    if 0 <= t + AHEAD - 1 < TILES:
                        exponential(r, t + AHEAD - 1)
                    if 0 <= t < TILES:
                        keep_low(r, t)
                    if t > 0 and t % UNIT == 0 and t <= TILES:
                        att_high(r, t // UNIT - 1)
                    if t < 0:
                        for n in (2 * t + 2 * AHEAD + 2, 2 * t + 2 * AHEAD + 3):
                            load_adj(r, n)
                    if 16 <= t < 16 + 4 * QT and t % 4 == 0:
                        load_adj(r, QT + (t - 16) // 4)
                    for o in range(O_ITEMS):
                        if o_slot(o) + 2 == t:
                            store(r, o)
                            if o + 2 < O_ITEMS:
                                load_x(r, o + 2)
                act.wait_ge(masks_made, r * (ROUND * QT) + ROUND * QT)
                act.wait_ge(summed, r * O_ITEMS + O_ITEMS)
                act.nop(nofuse=True)
            for n in range(4):
                act.wait_ge(z_free[n], 16 + ROUNDS * O_ITEMS // 4 * 16)

        @block.vector
        def _(dve):
            for n in range(2):
                dve.wait_ge(wo_in, 32 if n == 0 else 80)
                dve.wait_ge(wo_hi_done, n + 1)
                nc.vector.tensor_tensor(wo_lo[:, n, :, :], wo_raw[:, :, :], wo_hi[:, n, :, :].bitcast(F32),
                                        ALU.subtract).then_inc(wo_lo_done, 1)

            def mask_and_max(r, t):
                j, q = t // BT, t % QT
                if t % BT < QT:
                    dve.wait_ge(masks_made, r * (ROUND * QT) + (j * QT + q + 1))
                dve.wait_ge(scored, r * TILES + (t + 1))
                if t >= 4:
                    dve.wait_ge(transposed, r * (2 * TILES) + 2 * (t - 3))
                dve.nop(nofuse=True)
                nc.vector.tensor_tensor_reduce(out=prob[:, t % 4, :], in0=score[t % 2][:, :], in1=mask[:, j, q, :],
                                               scale=-SCALE, scalar=3e38, op0=ALU.add, op1=ALU.min,
                                               accum_out=neg_max[:, t % 4:t % 4 + 1]).then_inc(masked, 1)

            def invert(r, t):
                dve.wait_ge(exped, r * TILES + (t + 1))
                nc.vector.reciprocal(row_inv[:, t % 4:t % 4 + 1], row_sum[:, t % 4:t % 4 + 1]).then_inc(inverted, 1)

            def keep_high(r, t):
                dve.wait_ge(transposed, r * (2 * TILES) + (2 * t + 2))
                if t % UNIT == 0:
                    if t // UNIT >= 2:
                        dve.wait_ge(mixed_done, r * UNITS + (t // UNIT - 1))
                nc.vector.tensor_copy(turned_out(1, t), turned[1][:, :].rearrange("p (k n) -> p k n", k=4)
                                      ).then_inc(kept[1], 1)

            def att_low(r, u):
                dve.wait_ge(att_hi_done, r * (2 * UNITS) + 2 * (u + 1))
                for n in range(2):
                    last = nc.vector.tensor_tensor(att_part(att_lo, u, n), mixed[n * HD:(n + 1) * HD, 0:CH],
                                                   att_part(att_hi, u, n).bitcast(F32), ALU.subtract)
                last.then_inc(att_done, 1)

            def add_norm(r, o):
                dve.wait_ge(projected, r * O_ITEMS + (o + 1))
                nc.vector.tensor_tensor(y[:, :], outp[:, :], bias_o[:, :], ALU.add).then_inc(biased, 1)
                dve.wait_ge(biased, r * O_ITEMS + (o + 1))
                dve.wait_ge(x_in[o % 2], r * (O_ITEMS // 2 * 16) + (o // 2 + 1) * 16)
                dve.wait_ge(z_free[o % 4], r * (O_ITEMS // 4 * 16) + (o // 4 + 1) * 16)
                nc.vector.scalar_tensor_tensor(out=z[:, o % 4, :], in0=y[:, :], scalar=0.0, in1=x_res[:, o % 2, :],
                                               op0=ALU.max, op1=ALU.add).then_inc(summed, 1)
                dve.wait_ge(summed, r * O_ITEMS + (o + 1))
                nc.vector.bn_stats(out=stats[:, :], in_=z[:, o % 4, :]).then_inc(stat_done, 1)
                dve.wait_ge(stat_done, r * O_ITEMS + (o + 1))
                dve.nop(nofuse=True)
                nc.vector.bn_aggr(out=mean_var[:, o % 2, :], in_=stats[:, :]).then_inc(ready, 1)

            for n in range(4):
                dve.nop().then_inc(z_free[n], 16)
            with dve.Fori(0, ROUNDS) as r:
                for t in range(-AHEAD, TILES + 9):
                    if t + AHEAD < TILES:
                        mask_and_max(r, t + AHEAD)
                    if 0 <= t + AHEAD - 1 < TILES:
                        invert(r, t + AHEAD - 1)
                    if 0 <= t < TILES:
                        keep_high(r, t)
                    if t > 0 and t % UNIT == 0 and t <= TILES:
                        att_low(r, t // UNIT - 1)
                    for o in range(O_ITEMS):
                        if o_slot(o) == t:
                            add_norm(r, o)


def build(nc, x, adj, wq, bq, wk, bk, wv, bv, wo, bo, out):
    qk_parts = nc.dram_tensor("qk_parts", (BATCH, 4, D, N), F32R, kind="Internal").ap()
    v_all = nc.dram_tensor("v_all", (BATCH, N, D), F32, kind="Internal").ap()
    project(nc, x, wq, bq, wk, bk, wv, bv, qk_parts, v_all)
    attend(nc, x, adj, wo, bo, qk_parts, v_all, out)


_INS = ['x', 'adj', 'L0_gnn_Wq', 'L0_gnn_bq', 'L0_gnn_Wk', 'L0_gnn_bk', 'L0_gnn_Wv', 'L0_gnn_bv', 'L0_gnn_Wo',
        'L0_gnn_bo']


def kernel(**inputs):
    import numpy as _np
    import concourse.bacc as _bacc
    from concourse import mybir as _mybir
    from concourse.bass_utils import run_bass_kernel_spmd as _run

    nc = _bacc.Bacc("TRN2", target_bir_lowering=False, num_devices=1)
    arrays, args = {}, []
    for name in _INS:
        a = _np.ascontiguousarray(inputs[name])
        arrays[f"in_{name}_dram"] = a
        args.append(nc.dram_tensor(f"in_{name}_dram", a.shape, _mybir.dt.from_np(a.dtype), kind="ExternalInput").ap())
    out = nc.dram_tensor("out_0_dram", (BATCH, N, D), _mybir.dt.float32, kind="ExternalOutput").ap()
    build(nc, *args, out)
    r = _run(nc, [arrays], core_ids=[0])
    return r.results[0]["out_0_dram"]
```

```python
import concourse.bass as bass
from concourse import mybir
from contextlib import ExitStack

F32 = mybir.dt.float32
F32R = mybir.dt.float32r
BF16 = mybir.dt.bfloat16
I32 = mybir.dt.int32
ALU = mybir.AluOpType
ACT = mybir.ActivationFunctionType

P = 128
BATCH, N, D = 16, 1024, 512
HEADS = 8
HD = D // HEADS
PAIRS = HEADS // 2
KD = D // P
QT = N // P
HALF = 512
SCALE = HD ** -0.5
MASKED = -1e30
LN_EPS = 1e-5


def project(nc, x, wq, bq, wk, bk, wv, bv, qk_parts, v_all):
    XT_ITEMS, QK_ITEMS, V_ITEMS = QT, 2 * PAIRS * 2, QT
    ITEMS = XT_ITEMS + QK_ITEMS + V_ITEMS
    SPLITS = XT_ITEMS + QK_ITEMS
    BANKS = 8

    with ExitStack() as ctx:
        def sb(name, shape, dt):
            return ctx.enter_context(nc.sbuf_tensor(name, shape, dt))

        def sem(name):
            return ctx.enter_context(nc.semaphore(name))

        w_raw = sb("w_raw", [P, 3, KD, D], F32)
        w_hi = sb("w_hi", [P, 3, KD, D], F32R)
        w_lo = sb("w_lo", [P, 3, KD, D], F32R)
        bias_qk = sb("bias_qk", [P, 2, PAIRS], F32)
        bias_v = sb("bias_v", [P, D], F32)
        ident = sb("ident", [P, P], F32)
        x_in = sb("x_in", [P, QT, D], F32)
        xt_hi = sb("xt_hi", [P, KD, N], F32R)
        xt_lo = sb("xt_lo", [P, KD, N], F32R)
        out_hi = sb("out_hi", [P, 2, N], F32R)
        out_lo = sb("out_lo", [P, 2, N], F32R)
        out_v = sb("out_v", [P, 2, D], F32)
        bank = [ctx.enter_context(nc.psum_tensor(f"bank{n}", [P, HALF], F32)) for n in range(BANKS)]

        w_in = sem("w_in")
        w_hi_done = sem("w_hi_done")
        w_lo_done = sem("w_lo_done")
        ident_zero = sem("ident_zero")
        ident_done = sem("ident_done")
        x_loaded = sem("x_loaded")
        filled = sem("filled")
        hi_done = sem("hi_done")
        emptied = sem("emptied")
        qk_free = [sem(f"qk_free{n}") for n in range(2)]
        v_free = [sem(f"v_free{n}") for n in range(2)]

        block = ctx.enter_context(nc.Block())

        @block.gpsimd
        def _(pool):
            nc.gpsimd.memset(ident[:, :], 0.0).then_inc(ident_zero, 1)
            pool.wait_ge(ident_zero, 1)
            nc.gpsimd.affine_select(out=ident[:, :], in_=ident[:, :], compare_op=ALU.not_equal, fill=1.0,
                                    base=0, pattern=[[-1, P]], channel_multiplier=1).then_inc(ident_done, 1)
            pool.dma_start(x_in[:, :, :], x[0, :, :].rearrange("(t p) d -> p t d", p=P)).then_inc(x_loaded, 16)
            with pool.Fori(1, BATCH) as b:
                pool.wait_ge(filled, b * ITEMS - (ITEMS - XT_ITEMS))
                pool.dma_start(x_in[:, :, :],
                               x[bass.ds(b, 1), :, :].rearrange("o (t p) d -> p (o t) d", p=P)).then_inc(x_loaded, 16)

        @block.sync
        def _(sp):
            for n, w in enumerate((wq, wk, wv)):
                sp.dma_start(w_raw[:, n, :, :], w.rearrange("(k p) n -> p k n", p=P)).then_inc(w_in, 16)
            with nc.allow_non_contiguous_dma(reason="512 bias values, once"):
                for n, v in enumerate((bq, bk)):
                    sp.dma_start(bias_qk[:, n, :], v.rearrange("(g p) -> p g", p=P)).then_inc(w_in, 16)
            sp.dma_start(bias_v[:, :], bv.rearrange("(a n) -> a n", a=1).to_broadcast([P, D])).then_inc(w_in, 16)
            with sp.Fori(0, BATCH) as b:
                for g in range(2 * PAIRS):
                    which, pair = g // PAIRS, g % PAIRS
                    sp.wait_ge(emptied, b * ITEMS + (XT_ITEMS + 2 * g + 2))
                    for part, src in enumerate((out_hi, out_lo)):
                        sp.dma_start(qk_parts[bass.ds(b, 1), 2 * which + part, pair * P:(pair + 1) * P, :]
                                     .rearrange("o p n -> p (o n)").bitcast(F32),
                                     src[:, g % 2, :].bitcast(F32)).then_inc(qk_free[g % 2], 16)
                for t in range(V_ITEMS):
                    sp.wait_ge(emptied, b * ITEMS + (SPLITS + t + 1))
                    sp.dma_start(v_all[bass.ds(b, 1), t * P:(t + 1) * P, :].rearrange("o p n -> p (o n)"),
                                 out_v[:, t % 2, :]).then_inc(v_free[t % 2], 16)
            for n in range(2):
                sp.wait_ge(qk_free[n], 32 + BATCH * PAIRS * 32)
                sp.wait_ge(v_free[n], 16 + BATCH * V_ITEMS // 2 * 16)

        @block.tensor
        def _(pe):
            pe.wait_ge(ident_done, 1)
            pe.wait_ge(w_hi_done, 3)
            pe.wait_ge(w_lo_done, 3)

            def product(out, parts):
                terms = [(a, b, k) for a, b in ((0, 0), (0, 1), (1, 0)) for k in range(KD)]
                for n, (a, b, k) in enumerate(terms):
                    lhs, rhs = parts(a, b, k)
                    last = nc.tensor.matmul(out, lhs, rhs, start=n == 0, stop=n == len(terms) - 1)
                last.then_inc(filled, 1)

            xt, w = (xt_hi, xt_lo), (w_hi, w_lo)
            with pe.Fori(0, BATCH) as b:
                pe.wait_ge(x_loaded, b * 16 + 16)
                for t in range(XT_ITEMS):
                    for k in range(KD):
                        last = nc.tensor.transpose(bank[t][:, k * P:(k + 1) * P], x_in[:, t, k * P:(k + 1) * P],
                                                   ident[:, :])
                    last.then_inc(filled, 1)
                for n in range(QK_ITEMS):
                    item = XT_ITEMS + n
                    which, pair, half = n // (2 * PAIRS), n // 2 % PAIRS, n % 2
                    pe.wait_ge(emptied, b * ITEMS + max(item - BANKS + 1, (half + 1) * XT_ITEMS // 2))
                    product(bank[item % BANKS][:, :],
                            lambda i, j, k: (w[i][:, which, k, pair * P:(pair + 1) * P],
                                             xt[j][:, k, half * HALF:(half + 1) * HALF]))
                for t in range(V_ITEMS):
                    item = SPLITS + t
                    pe.wait_ge(emptied, b * ITEMS + (item - BANKS + 1))
                    product(bank[item % BANKS][:, :],
                            lambda i, j, k: (xt[i][:, k, t * P:(t + 1) * P], w[j][:, 2, k, :]))
                pe.wait_ge(emptied, b * ITEMS + ITEMS)
                pe.nop(nofuse=True)

        @block.scalar
        def _(act):
            for n in range(3):
                act.wait_ge(w_in, 6 * 16)
                nc.scalar.activation(w_hi[:, n, :, :], w_raw[:, n, :, :], ACT.Copy).then_inc(w_hi_done, 1)
            for n in range(2):
                act.nop().then_inc(qk_free[n], 32)
            with act.Fori(0, BATCH) as b:
                for t in range(XT_ITEMS):
                    act.wait_ge(filled, b * ITEMS + (t + 1))
                    nc.scalar.activation(xt_hi[:, :, t * P:(t + 1) * P],
                                         bank[t][:, :].rearrange("p (k n) -> p k n", k=KD),
                                         ACT.Copy).then_inc(hi_done, 1)
                for n in range(QK_ITEMS):
                    item = XT_ITEMS + n
                    g, half = n // 2, n % 2
                    which, pair = g // PAIRS, g % PAIRS
                    if half == 0:
                        act.wait_ge(qk_free[g % 2], b * (PAIRS * 32) + (g // 2 + 1) * 32)
                    act.wait_ge(filled, b * ITEMS + (item + 1))
                    nc.scalar.activation(out_hi[:, g % 2, half * HALF:(half + 1) * HALF], bank[item % BANKS][:, :],
                                         ACT.Identity, bias=bias_qk[:, which, pair:pair + 1]).then_inc(hi_done, 1)

        @block.vector
        def _(dve):
            dve.wait_ge(w_in, 6 * 16)
            for n in range(3):
                dve.wait_ge(w_hi_done, n + 1)
                nc.vector.tensor_tensor(w_lo[:, n, :, :], w_raw[:, n, :, :], w_hi[:, n, :, :].bitcast(F32),
                                        ALU.subtract).then_inc(w_lo_done, 1)
            for n in range(2):
                dve.nop().then_inc(v_free[n], 16)
            with dve.Fori(0, BATCH) as b:
                for t in range(XT_ITEMS):
                    dve.wait_ge(hi_done, b * SPLITS + (t + 1))
                    nc.vector.tensor_tensor(xt_lo[:, :, t * P:(t + 1) * P],
                                            bank[t][:, :].rearrange("p (k n) -> p k n", k=KD),
                                            xt_hi[:, :, t * P:(t + 1) * P].bitcast(F32),
                                            ALU.subtract).then_inc(emptied, 1)
                for n in range(QK_ITEMS):
                    item = XT_ITEMS + n
                    g, half = n // 2, n % 2
                    which, pair = g // PAIRS, g % PAIRS
                    cols = slice(half * HALF, (half + 1) * HALF)
                    dve.wait_ge(hi_done, b * SPLITS + (item + 1))
                    nc.vector.scalar_tensor_tensor(out=out_lo[:, g % 2, cols], in0=bank[item % BANKS][:, :],
                                                   scalar=bias_qk[:, which, pair:pair + 1],
                                                   in1=out_hi[:, g % 2, cols].bitcast(F32),
                                                   op0=ALU.add, op1=ALU.subtract).then_inc(emptied, 1)
                for t in range(V_ITEMS):
                    item = SPLITS + t
                    dve.wait_ge(v_free[t % 2], b * (V_ITEMS // 2 * 16) + (t // 2 + 1) * 16)
                    dve.wait_ge(filled, b * ITEMS + (item + 1))
                    nc.vector.tensor_tensor(out_v[:, t % 2, :], bank[item % BANKS][:, :], bias_v[:, :],
                                            ALU.add).then_inc(emptied, 1)


def attend(nc, x, adj, wo, bo, qk_parts, v_all, out):
    ROUND = 2
    ROUNDS = BATCH // ROUND
    FIRST, LAST = 0, ROUNDS - 1
    BT = HEADS * QT
    TILES = ROUND * BT
    UNIT = 4
    UNITS = TILES // UNIT
    BU = BT // UNIT
    ALL_HEADS = ROUND * HEADS
    ALL_PAIRS = ROUND * PAIRS
    MASKS = ROUND * QT
    OUTS = ROUND * QT
    AHEAD = 3
    TAIL = 16
    CH = UNIT // 2 * P
    RING = 4

    def out_slot(o):
        return (o // QT + 1) * BT + 11 * (o % QT) // 8

    def mask_slot(n):
        return (n // QT - 1) * BT + 4 + 4 * (n % QT)

    def outs_of(r, t, shift=0):
        return [o for o in range(-OUTS if r is not FIRST else 0, OUTS)
                if out_slot(o) + shift == t]

    def masks_of(r, t, shift=0):
        return [n for n in range(QT, MASKS + QT if r is not LAST else MASKS) if mask_slot(n) + shift == t]

    def until(engine, sem, r, per, count):
        if not isinstance(r, int):
            engine.wait_ge(sem, r * per + count)
        elif r * per + count > 0:
            engine.wait_ge(sem, r * per + count)

    def rounds(engine, slot):
        for t in range(-AHEAD, TILES):
            slot(FIRST, t)
        with engine.Fori(1, LAST) as r:
            for t in range(TILES):
                slot(r, t)
        for t in range(TILES + TAIL):
            slot(LAST, t)

    def there(r, n, per):
        return not (r is FIRST and n < 0) and not (r is LAST and n >= per)

    with ExitStack() as ctx:
        def sb(name, shape, dt):
            return ctx.enter_context(nc.sbuf_tensor(name, shape, dt))

        def pb(name, shape, dt):
            return ctx.enter_context(nc.psum_tensor(name, shape, dt))

        def sem(name):
            return ctx.enter_context(nc.semaphore(name))

        wo_hi = sb("wo_hi", [P, 2, PAIRS, D], F32R)
        wo_lo = sb("wo_lo", [P, 2, PAIRS, D], F32R)
        bias_o = sb("bias_o", [P, D], F32)
        ident = sb("ident2", [P, P], F32)
        q_stack = sb("q_stack", [P, 2, N], F32R)
        k_hi = sb("k_hi", [P, 2, N], F32R)
        k_lo = sb("k_lo", [P, 2, N], F32R)
        v_pair = sb("v_pair", [P, 2, QT, P], F32)
        adj_in = sb("adj_in", [P, 2, N], I32)
        mask = sb("mask", [P, ROUND, QT, N], BF16)
        prob = sb("prob", [P, RING, N], F32)
        wo_raw = prob[:, 0:2, :].rearrange("p a (g n) -> p (a g) n", g=2)
        neg_max = sb("neg_max", [P, RING], F32)
        row_sum = sb("row_sum", [P, RING], F32)
        row_inv = sb("row_inv", [P, RING], F32)
        prob_t = sb("prob_t", [P, 2, QT, 2, CH], F32)
        att_hi = sb("att_hi", [P, PAIRS, 2, 2, CH], F32R)
        att_lo = sb("att_lo", [P, PAIRS, 2, 2, CH], F32R)
        x_res = sb("x_res", [P, RING, D], F32)
        y = sb("y", [P, D], F32)
        z = sb("z", [P, RING, D], F32)
        stats = sb("stats", [P, 6], F32)
        mean_var = sb("mean_var", [P, RING, 2], F32)
        half_power = sb("half_power", [P, 1], F32)
        var_eps = sb("var_eps", [P, 1], F32)
        inv_std = sb("inv_std", [P, 1], F32)

        score = [pb(f"score{n}", [P, N], F32) for n in range(2)]
        turned = [pb(f"turned{n}", [P, HALF], F32) for n in range(2)]
        mixed = pb("mixed", [P, HALF], F32)
        outp = pb("outp", [P, HALF], F32)

        wo_in = sem("wo_in")
        wo_hi_done = sem("wo_hi_done")
        wo_lo_done = sem("wo_lo_done")
        ident_zero = sem("ident2_zero")
        ident_done = sem("ident2_done")
        head_in = [sem(f"head_in{n}") for n in range(2)]
        v_in = [sem(f"v_in{n}") for n in range(2)]
        adj_in_done = [sem(f"adj_in_done{n}") for n in range(2)]
        x_in = [sem(f"x_in{n}") for n in range(RING)]
        masks_made = sem("masks_made")
        scored = sem("scored")
        masked = sem("masked")
        exped = sem("exped")
        inverted = sem("inverted")
        normed = sem("normed")
        transposed = sem("transposed")
        kept = [sem("kept_low"), sem("kept_high")]
        mixed_done = sem("mixed_done")
        att_hi_done = sem("att_hi_done")
        att_done = sem("att_done")
        projected = sem("projected")
        biased = sem("biased")
        summed = sem("summed")
        stat_done = sem("stat_done")
        ready = sem("ready")
        var_done = sem("var_done")
        std_done = sem("std_done")
        finished = sem("finished")
        z_free = [sem(f"z_free{n}") for n in range(RING)]

        block = ctx.enter_context(nc.Block())

        def batch_rows(t, r, n):
            b = r * ROUND + n // QT
            where = slice(b, b + 1) if isinstance(b, int) else bass.ds(b, 1)
            q = n % QT
            return t[where, q * P:(q + 1) * P, :].rearrange("o p n -> p (o n)")

        @block.sync
        def _(sp):
            for n in range(2):
                if n:
                    sp.wait_ge(wo_lo_done, n)
                for h in range(2):
                    sp.dma_start(wo_raw[h * HD:(h + 1) * HD, :, :],
                                 wo.rearrange("(g two p) n -> two p g n", two=2, p=HD)[(h + n) % 2, :, :, :]
                                 ).then_inc(wo_in, 16)
            sp.dma_start(bias_o[:, :], bo.rearrange("(a n) -> a n", a=1).to_broadcast([P, D])).then_inc(wo_in, 16)


            def load_head(r, h):
                until(sp, scored, r, TILES, (h - 1) * QT)
                sp.nop(nofuse=True)
                b, rows = r * ROUND + h // HEADS, slice(h % HEADS * HD, (h % HEADS + 1) * HD)
                where = slice(b, b + 1) if isinstance(b, int) else bass.ds(b, 1)
                for dst, parts in ((q_stack, (0, 1)), (k_hi, (2, 2)), (k_lo, (3, 3))):
                    for n, part in enumerate(parts):
                        sp.dma_start(dst[n * HD:(n + 1) * HD, h % 2, :].bitcast(F32),
                                     qk_parts[where, part, rows, :].rearrange("o p n -> p (o n)").bitcast(F32)
                                     ).then_inc(head_in[h % 2], 16)

            def load_v(r, pair):
                until(sp, mixed_done, r, UNITS, (pair - 1) * 4)
                sp.nop(nofuse=True)
                b, cols = r * ROUND + pair // PAIRS, slice(pair % PAIRS * P, (pair % PAIRS + 1) * P)
                where = slice(b, b + 1) if isinstance(b, int) else bass.ds(b, 1)
                sp.dma_start(v_pair[:, pair % 2, :, :],
                             v_all[where, :, cols].rearrange("o (t p) d -> p (o t) d", p=P)
                             ).then_inc(v_in[pair % 2], 16)

            def load_adj(r, n):
                until(sp, masks_made, r, MASKS, n - 1)
                sp.nop(nofuse=True)
                sp.dma_start(adj_in[:, n % 2, :], batch_rows(adj, r, n)).then_inc(adj_in_done[n % 2], 16)

            def load_x(r, o):
                until(sp, summed, r, OUTS, o - (RING - 1))
                sp.nop(nofuse=True)
                sp.dma_start(x_res[:, o % RING, :], batch_rows(x, r, o)).then_inc(x_in[o % RING], 16)

            def store(r, o):
                until(sp, finished, r, OUTS, o + 1)
                sp.nop(nofuse=True)
                sp.dma_start(batch_rows(out, r, o), z[:, o % RING, :]).then_inc(z_free[o % RING], 16)

            load_adj(FIRST, 0)
            load_head(FIRST, 0)
            for n in range(1, QT):
                load_adj(FIRST, n)
            load_v(FIRST, 0)

            def slot(r, t):
                h, pair = (t + AHEAD) // QT + 1, (t - UNIT) // (2 * QT) + 1
                if (t + AHEAD) % QT == 0 and there(r, h, ALL_HEADS):
                    load_head(r, h)
                if (t - UNIT) % (2 * QT) == 0 and there(r, pair, ALL_PAIRS):
                    load_v(r, pair)
                for n in masks_of(r, t, -3):
                    load_adj(r, n)
                for o in outs_of(r, t, -3):
                    load_x(r, o)
                for o in outs_of(r, t, 3):
                    store(r, o)

            rounds(sp, slot)
            for n in range(RING):
                sp.wait_ge(z_free[n], 16 + ROUNDS * OUTS // RING * 16)

        @block.gpsimd
        def _(pool):
            nc.gpsimd.memset(ident[:, :], 0.0).then_inc(ident_zero, 1)
            pool.wait_ge(ident_zero, 1)
            nc.gpsimd.affine_select(out=ident[:, :], in_=ident[:, :], compare_op=ALU.not_equal, fill=1.0,
                                    base=0, pattern=[[-1, P]], channel_multiplier=1).then_inc(ident_done, 1)
            nc.gpsimd.memset(half_power[:, :], -0.5).then_inc(ident_done, 1)


            def make_mask(r, n):
                until(pool, adj_in_done[n % 2], r, MASKS // 2 * 16, (n // 2 + 1) * 16)
                until(pool, masked, r, TILES, (n // QT - 1) * BT)
                pool.nop(nofuse=True)
                nc.gpsimd.tensor_scalar(mask[:, n // QT % 2, n % QT, :], adj_in[:, n % 2, :], 0.0, MASKED,
                                        ALU.is_le, ALU.mult).then_inc(masks_made, 1)

            def normalise(r, t):
                until(pool, inverted, r, TILES, t + 1)
                pool.nop(nofuse=True)
                nc.gpsimd.tensor_scalar(prob[:, t % RING, :], prob[:, t % RING, :],
                                        row_inv[:, t % RING:t % RING + 1], 1.0,
                                        ALU.mult, ALU.mult).then_inc(normed, 1)

            def finish(r, o):
                until(pool, ready, r, OUTS, o + 1)
                pool.nop(nofuse=True)
                nc.gpsimd.tensor_scalar(var_eps[:, :], mean_var[:, o % RING, 1:2], LN_EPS, None,
                                        ALU.add).then_inc(var_done, 1)
                until(pool, var_done, r, OUTS, o + 1)
                nc.gpsimd.tensor_tensor(inv_std[:, :], var_eps[:, :], half_power[:, :], ALU.pow).then_inc(std_done, 1)
                until(pool, std_done, r, OUTS, o + 1)
                pool.nop(nofuse=True)
                nc.gpsimd.tensor_scalar(z[:, o % RING, :], z[:, o % RING, :], mean_var[:, o % RING, 0:1],
                                        inv_std[:, :], ALU.subtract, ALU.mult).then_inc(finished, 1)

            pool.wait_ge(ident_done, 2)
            for n in range(4):
                make_mask(FIRST, n)

            def slot(r, t):
                for o in outs_of(r, t, 1):
                    finish(r, o)
                if there(r, t + AHEAD - 1, TILES):
                    normalise(r, t + AHEAD - 1)
                if r is FIRST and 4 <= t + AHEAD + 3 < QT:
                    make_mask(r, t + AHEAD + 3)
                for n in masks_of(r, t):
                    make_mask(r, n)

            rounds(pool, slot)

        @block.tensor
        def _(pe):
            pe.wait_ge(ident_done, 2)
            pe.wait_ge(wo_lo_done, 2)

            def scores(r, t):
                h, q = t // QT, t % QT
                buf = h % 2
                if q == 0:
                    until(pe, head_in[buf], r, ALL_HEADS // 2 * 96, (h // 2 + 1) * 96)
                until(pe, masked, r, TILES, t - 1)
                for n, k in enumerate((k_hi, k_lo)):
                    for half in range(2):
                        cols = slice(half * HALF, (half + 1) * HALF)
                        last = nc.tensor.matmul(score[t % 2][:, cols], q_stack[:, buf, q * P:(q + 1) * P],
                                                k[:, buf, cols], start=n == 0, stop=n == 1)
                last.then_inc(scored, 1)

            def turn(r, t):
                until(pe, normed, r, TILES, t + 1)
                for half in range(2):
                    until(pe, kept[half], r, TILES, t)
                    for n in range(4):
                        k = half * 4 + n
                        last = nc.tensor.transpose(turned[half][:, n * P:(n + 1) * P],
                                                   prob[:, t % RING, k * P:(k + 1) * P], ident[:, :])
                    last.then_inc(transposed, 1)

            def mix(r, u, part):
                h = u * UNIT // QT
                pair = h // 2
                if part == 0:
                    if u % 4 == 0:
                        until(pe, v_in[pair % 2], r, ALL_PAIRS // 2 * 16, (pair // 2 + 1) * 16)
                    for half in range(2):
                        until(pe, kept[half], r, TILES, (u + 1) * UNIT)
                    until(pe, att_done, r, UNITS, u)
                for k in (2 * part, 2 * part + 1):
                    for n in range(2):
                        chunk = n if h % 2 == 0 else 1 - n
                        last = nc.tensor.matmul(mixed[n * HD:(n + 1) * HD, 0:CH],
                                                v_pair[:, pair % 2, k, h % 2 * HD:(h % 2 + 1) * HD],
                                                prob_t[:, u % 2, k, chunk, :], start=k == 0, stop=k == QT - 1)
                if part == UNIT - 1:
                    last.then_inc(mixed_done, 1)

            def project_out(r, o):
                q = o % QT
                of_head, chunk, off = q // 4, q % 4 // 2, q % 2 * P
                until(pe, att_done, r, UNITS, (o // QT + 1) * BU - 1 + of_head)
                until(pe, biased, r, OUTS, o)
                att, w = (att_hi, att_lo), (wo_hi, wo_lo)
                terms = [(a, c, g) for a, c in ((0, 0), (0, 1), (1, 0)) for g in range(PAIRS)]
                for n, (a, c, g) in enumerate(terms):
                    last = nc.tensor.matmul(outp[:, :], att[a][:, g, of_head, chunk, off:off + P],
                                            w[c][:, chunk, g, :], start=n == 0, stop=n == len(terms) - 1)
                last.then_inc(projected, 1)

            def slot(r, t):
                u, part = t // UNIT - 1, t % UNIT
                if there(r, t + AHEAD, TILES):
                    scores(r, t + AHEAD)
                if t >= 0 and there(r, t, TILES):
                    turn(r, t)
                if there(r, u, UNITS):
                    mix(r, u, part)
                for o in outs_of(r, t):
                    project_out(r, o)

            rounds(pe, slot)

        def turned_out(half, t):
            in_unit = t % UNIT
            off = in_unit % 2 * P
            return prob_t[:, t // UNIT % 2, half * 4:half * 4 + 4, in_unit // 2, off:off + P]

        def att_part(att, u, n):
            h = u * UNIT // QT
            chunk = n if h % 2 == 0 else 1 - n
            return att[n * HD:(n + 1) * HD, h % HEADS // 2, u % 2, chunk, :]

        @block.scalar
        def _(act):
            for n in range(2):
                act.wait_ge(wo_in, 32 if n == 0 else 80)
                nc.scalar.activation(wo_hi[:, n, :, :], wo_raw[:, :, :], ACT.Copy).then_inc(wo_hi_done, 1)

            def exponential(r, t):
                until(act, masked, r, TILES, t + 1)
                nc.scalar.activation(prob[:, t % RING, :], prob[:, t % RING, :], ACT.Exp,
                                     bias=neg_max[:, t % RING:t % RING + 1], scale=-1.0,
                                     accum_out=row_sum[:, t % RING:t % RING + 1]).then_inc(exped, 1)

            def keep_low(r, t):
                until(act, transposed, r, 2 * TILES, 2 * t + 1)
                if t % UNIT == 0:
                    until(act, mixed_done, r, UNITS, t // UNIT - 1)
                nc.scalar.activation(turned_out(0, t), turned[0][:, :].rearrange("p (k n) -> p k n", k=4),
                                     ACT.Copy).then_inc(kept[0], 1)

            def att_high(r, u):
                until(act, mixed_done, r, UNITS, u + 1)
                if u % BU < 2:
                    until(act, projected, r, OUTS, (u // BU - 1) * QT + (u % 2 + 1) * 4)
                for n in range(2):
                    nc.scalar.activation(att_part(att_hi, u, n), mixed[n * HD:(n + 1) * HD, 0:CH],
                                         ACT.Copy).then_inc(att_hi_done, 1)

            def slot(r, t):
                u = t // UNIT - 2
                if t % UNIT == 0 and there(r, u, UNITS):
                    att_high(r, u)
                if there(r, t + AHEAD - 1, TILES):
                    exponential(r, t + AHEAD - 1)
                if t >= 0 and there(r, t, TILES):
                    keep_low(r, t)

            rounds(act, slot)

        @block.vector
        def _(dve):
            for n in range(2):
                dve.wait_ge(wo_in, 32 if n == 0 else 80)
                dve.wait_ge(wo_hi_done, n + 1)
                nc.vector.tensor_tensor(wo_lo[:, n, :, :], wo_raw[:, :, :], wo_hi[:, n, :, :].bitcast(F32),
                                        ALU.subtract).then_inc(wo_lo_done, 1)

            def mask_and_max(r, t):
                j, q = t // BT, t % QT
                if t % BT < QT:
                    until(dve, masks_made, r, MASKS, j * QT + q + 1)
                until(dve, scored, r, TILES, t + 1)
                until(dve, transposed, r, 2 * TILES, 2 * (t - (RING - 1)))
                dve.nop(nofuse=True)
                nc.vector.tensor_tensor_reduce(out=prob[:, t % RING, :], in0=score[t % 2][:, :],
                                               in1=mask[:, j % 2, q, :], scale=-SCALE, scalar=3e38,
                                               op0=ALU.add, op1=ALU.min,
                                               accum_out=neg_max[:, t % RING:t % RING + 1]).then_inc(masked, 1)

            def invert(r, t):
                until(dve, exped, r, TILES, t + 1)
                nc.vector.reciprocal(row_inv[:, t % RING:t % RING + 1],
                                     row_sum[:, t % RING:t % RING + 1]).then_inc(inverted, 1)

            def keep_high(r, t):
                until(dve, transposed, r, 2 * TILES, 2 * t + 2)
                if t % UNIT == 0:
                    until(dve, mixed_done, r, UNITS, t // UNIT - 1)
                nc.vector.tensor_copy(turned_out(1, t), turned[1][:, :].rearrange("p (k n) -> p k n", k=4)
                                      ).then_inc(kept[1], 1)

            def att_low(r, u):
                until(dve, att_hi_done, r, 2 * UNITS, 2 * (u + 1))
                for n in range(2):
                    last = nc.vector.tensor_tensor(att_part(att_lo, u, n), mixed[n * HD:(n + 1) * HD, 0:CH],
                                                   att_part(att_hi, u, n).bitcast(F32), ALU.subtract)
                last.then_inc(att_done, 1)

            def add_norm(r, o):
                until(dve, projected, r, OUTS, o + 1)
                nc.vector.tensor_tensor(y[:, :], outp[:, :], bias_o[:, :], ALU.add).then_inc(biased, 1)
                until(dve, biased, r, OUTS, o + 1)
                until(dve, x_in[o % RING], r, OUTS // RING * 16, (o // RING + 1) * 16)
                until(dve, z_free[o % RING], r, OUTS // RING * 16, (o // RING + 1) * 16)
                nc.vector.scalar_tensor_tensor(out=z[:, o % RING, :], in0=y[:, :], scalar=0.0,
                                               in1=x_res[:, o % RING, :],
                                               op0=ALU.max, op1=ALU.add).then_inc(summed, 1)
                until(dve, summed, r, OUTS, o + 1)
                nc.vector.bn_stats(out=stats[:, :], in_=z[:, o % RING, :]).then_inc(stat_done, 1)
                until(dve, stat_done, r, OUTS, o + 1)
                dve.nop(nofuse=True)
                nc.vector.bn_aggr(out=mean_var[:, o % RING, :], in_=stats[:, :]).then_inc(ready, 1)

            for n in range(RING):
                dve.nop().then_inc(z_free[n], 16)

            def slot(r, t):
                u = t // UNIT - 2
                if t % UNIT == 0 and there(r, u, UNITS):
                    att_low(r, u)
                if there(r, t + AHEAD, TILES):
                    mask_and_max(r, t + AHEAD)
                if there(r, t + AHEAD - 1, TILES):
                    invert(r, t + AHEAD - 1)
                if t >= 0 and there(r, t, TILES):
                    keep_high(r, t)
                for o in outs_of(r, t):
                    add_norm(r, o)

            rounds(dve, slot)


def build(nc, x, adj, wq, bq, wk, bk, wv, bv, wo, bo, out):
    qk_parts = nc.dram_tensor("qk_parts", (BATCH, 4, D, N), F32R, kind="Internal").ap()
    v_all = nc.dram_tensor("v_all", (BATCH, N, D), F32, kind="Internal").ap()
    project(nc, x, wq, bq, wk, bk, wv, bv, qk_parts, v_all)
    attend(nc, x, adj, wo, bo, qk_parts, v_all, out)


_INS = ['x', 'adj', 'L0_gnn_Wq', 'L0_gnn_bq', 'L0_gnn_Wk', 'L0_gnn_bk', 'L0_gnn_Wv', 'L0_gnn_bv', 'L0_gnn_Wo',
        'L0_gnn_bo']


def kernel(**inputs):
    import numpy as _np
    import concourse.bacc as _bacc
    from concourse import mybir as _mybir
    from concourse.bass_utils import run_bass_kernel_spmd as _run

    nc = _bacc.Bacc("TRN2", target_bir_lowering=False, num_devices=1)
    arrays, args = {}, []
    for name in _INS:
        a = _np.ascontiguousarray(inputs[name])
        arrays[f"in_{name}_dram"] = a
        args.append(nc.dram_tensor(f"in_{name}_dram", a.shape, _mybir.dt.from_np(a.dtype), kind="ExternalInput").ap())
    out = nc.dram_tensor("out_0_dram", (BATCH, N, D), _mybir.dt.float32, kind="ExternalOutput").ap()
    build(nc, *args, out)
    r = _run(nc, [arrays], core_ids=[0])
    return r.results[0]["out_0_dram"]
```

```python
import concourse.bass as bass
from concourse import mybir
from contextlib import ExitStack

F32 = mybir.dt.float32
F32R = mybir.dt.float32r
BF16 = mybir.dt.bfloat16
I32 = mybir.dt.int32
ALU = mybir.AluOpType
ACT = mybir.ActivationFunctionType

P = 128
BATCH, N, D = 16, 1024, 512
HEADS = 8
HD = D // HEADS
PAIRS = HEADS // 2
KD = D // P
QT = N // P
HALF = 512
SCALE = HD ** -0.5
MASKED = -1e30
LN_EPS = 1e-5


def until(engine, sem, r, per, count):
    if not isinstance(r, int):
        engine.wait_ge(sem, r * per + count)
    elif r * per + count > 0:
        engine.wait_ge(sem, r * per + count)


def project(nc, x, wq, bq, wk, bk, wv, bv, qk_all, v_all):
    XT_ITEMS, QK_ITEMS, V_ITEMS = QT, 2 * PAIRS * 2, QT
    ITEMS = XT_ITEMS + QK_ITEMS + V_ITEMS
    BANKS = 8

    with ExitStack() as ctx:
        def sb(name, shape, dt):
            return ctx.enter_context(nc.sbuf_tensor(name, shape, dt))

        def sem(name):
            return ctx.enter_context(nc.semaphore(name))

        w_raw = sb("w_raw", [P, 3, KD, D], F32)
        w_hi = sb("w_hi", [P, 3, KD, D], F32R)
        w_lo = sb("w_lo", [P, 3, KD, D], F32R)
        bias_qk = sb("bias_qk", [P, 2, PAIRS], F32)
        bias_v = sb("bias_v", [P, D], F32)
        ident = sb("ident", [P, P], F32)
        x_in = sb("x_in", [P, QT, D], F32)
        xt_hi = sb("xt_hi", [P, KD, N], F32R)
        xt_lo = sb("xt_lo", [P, KD, N], F32R)
        out_qk = sb("out_qk", [P, 2, N], F32)
        out_v = sb("out_v", [P, 2, D], F32)
        bank = [ctx.enter_context(nc.psum_tensor(f"bank{n}", [P, HALF], F32)) for n in range(BANKS)]

        w_in = [sem(f"w_in{n}") for n in range(3)]
        bias_in = sem("bias_in")
        w_hi_done = sem("w_hi_done")
        w_lo_done = sem("w_lo_done")
        ident_zero = sem("ident_zero")
        ident_done = sem("ident_done")
        first_x = [sem(f"first_x{n}") for n in range(2)]
        x_loaded = sem("x_loaded")
        filled = sem("filled")
        hi_done = sem("hi_done")
        emptied = sem("emptied")
        qk_free = [sem(f"qk_free{n}") for n in range(2)]
        v_free = [sem(f"v_free{n}") for n in range(2)]

        block = ctx.enter_context(nc.Block())

        @block.gpsimd
        def _(pool):
            nc.gpsimd.memset(ident[:, :], 0.0).then_inc(ident_zero, 1)
            pool.wait_ge(ident_zero, 1)
            nc.gpsimd.affine_select(out=ident[:, :], in_=ident[:, :], compare_op=ALU.not_equal, fill=1.0,
                                    base=0, pattern=[[-1, P]], channel_multiplier=1).then_inc(ident_done, 1)
            with pool.Fori(1, BATCH) as b:
                pool.wait_ge(filled, b * ITEMS - (ITEMS - XT_ITEMS))
                pool.dma_start(x_in[:, :, :],
                               x[bass.ds(b, 1), :, :].rearrange("o (t p) d -> p (o t) d", p=P)).then_inc(x_loaded, 16)

        @block.sync
        def _(sp):
            def load_first_x(half):
                rows, tiles = slice(half * HALF, (half + 1) * HALF), slice(half * QT // 2, (half + 1) * QT // 2)
                sp.dma_start(x_in[:, tiles, :], x[0, rows, :].rearrange("(t p) d -> p t d", p=P)
                             ).then_inc(first_x[half], 16)

            load_first_x(0)
            for n, w in enumerate((wq, wk, wv)):
                sp.dma_start(w_raw[:, n, :, :], w.rearrange("(k p) n -> p k n", p=P)).then_inc(w_in[n], 16)
                if n == 0:
                    load_first_x(1)
            with nc.allow_non_contiguous_dma(reason="512 bias values, once"):
                for n, v in enumerate((bq, bk)):
                    sp.dma_start(bias_qk[:, n, :], v.rearrange("(g p) -> p g", p=P)).then_inc(bias_in, 16)
            sp.dma_start(bias_v[:, :], bv.rearrange("(a n) -> a n", a=1).to_broadcast([P, D])).then_inc(bias_in, 16)
            with sp.Fori(0, BATCH) as b:
                for g in range(2 * PAIRS):
                    which, pair = g // PAIRS, g % PAIRS
                    sp.wait_ge(emptied, b * ITEMS + (XT_ITEMS + 2 * g + 2))
                    sp.dma_start(qk_all[bass.ds(b, 1), which, pair * P:(pair + 1) * P, :]
                                 .rearrange("o p n -> p (o n)"),
                                 out_qk[:, g % 2, :]).then_inc(qk_free[g % 2], 16)
                for t in range(V_ITEMS):
                    sp.wait_ge(emptied, b * ITEMS + (XT_ITEMS + QK_ITEMS + t + 1))
                    sp.dma_start(v_all[bass.ds(b, 1), t * P:(t + 1) * P, :].rearrange("o p n -> p (o n)"),
                                 out_v[:, t % 2, :]).then_inc(v_free[t % 2], 16)
            for n in range(2):
                sp.wait_ge(qk_free[n], 16 + BATCH * PAIRS * 16)
                sp.wait_ge(v_free[n], 16 + BATCH * V_ITEMS // 2 * 16)

        @block.tensor
        def _(pe):
            pe.wait_ge(ident_done, 1)

            def product(out, parts):
                terms = [(a, b, k) for a, b in ((0, 0), (0, 1), (1, 0)) for k in range(KD)]
                for n, (a, b, k) in enumerate(terms):
                    lhs, rhs = parts(a, b, k)
                    last = nc.tensor.matmul(out, lhs, rhs, start=n == 0, stop=n == len(terms) - 1)
                last.then_inc(filled, 1)

            xt, w = (xt_hi, xt_lo), (w_hi, w_lo)

            def batch(b):
                if not isinstance(b, int):
                    pe.wait_ge(x_loaded, b * 16)
                for t in range(XT_ITEMS):
                    if isinstance(b, int) and t % (XT_ITEMS // 2) == 0:
                        pe.wait_ge(first_x[t // (XT_ITEMS // 2)], 16)
                    until(pe, emptied, b, ITEMS, t - BANKS + 1)
                    for k in range(KD):
                        last = nc.tensor.transpose(bank[t][:, k * P:(k + 1) * P], x_in[:, t, k * P:(k + 1) * P],
                                                   ident[:, :])
                    last.then_inc(filled, 1)
                for n in range(QK_ITEMS):
                    item = XT_ITEMS + n
                    which, pair, half = n // (2 * PAIRS), n // 2 % PAIRS, n % 2
                    if n % (2 * PAIRS) == 0:
                        pe.wait_ge(w_lo_done, which + 1)
                    until(pe, emptied, b, ITEMS, max(item - BANKS + 1, (half + 1) * XT_ITEMS // 2))
                    product(bank[item % BANKS][:, :],
                            lambda i, j, k: (w[i][:, which, k, pair * P:(pair + 1) * P],
                                             xt[j][:, k, half * HALF:(half + 1) * HALF]))
                pe.wait_ge(w_lo_done, 3)
                for t in range(V_ITEMS):
                    item = XT_ITEMS + QK_ITEMS + t
                    until(pe, emptied, b, ITEMS, item - BANKS + 1)
                    product(bank[item % BANKS][:, :],
                            lambda i, j, k: (xt[i][:, k, t * P:(t + 1) * P], w[j][:, 2, k, :]))

            batch(0)
            with pe.Fori(1, BATCH) as b:
                batch(b)

        @block.scalar
        def _(act):
            def split_weight(n):
                act.wait_ge(w_in[n], 16)
                nc.scalar.activation(w_hi[:, n, :, :], w_raw[:, n, :, :], ACT.Copy).then_inc(w_hi_done, 1)

            def batch(b):
                for t in range(XT_ITEMS):
                    if isinstance(b, int) and t == XT_ITEMS // 2:
                        split_weight(0)
                    until(act, filled, b, ITEMS, t + 1)
                    nc.scalar.activation(xt_hi[:, :, t * P:(t + 1) * P],
                                         bank[t][:, :].rearrange("p (k n) -> p k n", k=KD),
                                         ACT.Copy).then_inc(hi_done, 1)
                if isinstance(b, int):
                    split_weight(1)
                    split_weight(2)

            batch(0)
            with act.Fori(1, BATCH) as b:
                batch(b)

        @block.vector
        def _(dve):
            for n in range(2):
                dve.nop().then_inc(qk_free[n], 16)
                dve.nop().then_inc(v_free[n], 16)

            def split_weight(n):
                dve.wait_ge(w_hi_done, n + 1)
                nc.vector.tensor_tensor(w_lo[:, n, :, :], w_raw[:, n, :, :], w_hi[:, n, :, :].bitcast(F32),
                                        ALU.subtract).then_inc(w_lo_done, 1)

            def batch(b):
                for t in range(XT_ITEMS):
                    if isinstance(b, int) and t == XT_ITEMS // 2:
                        split_weight(0)
                    until(dve, hi_done, b, XT_ITEMS, t + 1)
                    nc.vector.tensor_tensor(xt_lo[:, :, t * P:(t + 1) * P],
                                            bank[t][:, :].rearrange("p (k n) -> p k n", k=KD),
                                            xt_hi[:, :, t * P:(t + 1) * P].bitcast(F32),
                                            ALU.subtract).then_inc(emptied, 1)
                if isinstance(b, int):
                    split_weight(1)
                    split_weight(2)
                    dve.wait_ge(bias_in, 48)
                for n in range(QK_ITEMS):
                    item = XT_ITEMS + n
                    g, half = n // 2, n % 2
                    which, pair = g // PAIRS, g % PAIRS
                    if half == 0:
                        until(dve, qk_free[g % 2], b, PAIRS * 16, (g // 2 + 1) * 16)
                    until(dve, filled, b, ITEMS, item + 1)
                    nc.vector.tensor_scalar(out_qk[:, g % 2, half * HALF:(half + 1) * HALF],
                                            bank[item % BANKS][:, :], bias_qk[:, which, pair:pair + 1], None,
                                            ALU.add).then_inc(emptied, 1)
                for t in range(V_ITEMS):
                    item = XT_ITEMS + QK_ITEMS + t
                    until(dve, v_free[t % 2], b, V_ITEMS // 2 * 16, (t // 2 + 1) * 16)
                    until(dve, filled, b, ITEMS, item + 1)
                    nc.vector.tensor_tensor(out_v[:, t % 2, :], bank[item % BANKS][:, :], bias_v[:, :],
                                            ALU.add).then_inc(emptied, 1)

            batch(0)
            with dve.Fori(1, BATCH) as b:
                batch(b)


def attend(nc, x, adj, wo, bo, qk_all, v_all, out):
    ROUND = 2
    ROUNDS = BATCH // ROUND
    FIRST, LAST = 0, ROUNDS - 1
    BT = HEADS * QT
    TILES = ROUND * BT
    UNIT = 4
    PARTS = 2
    UNITS = TILES // UNIT
    BU = BT // UNIT
    ALL_HEADS = ROUND * HEADS
    ALL_PAIRS = ROUND * PAIRS
    MASKS = ROUND * QT
    OUTS = ROUND * QT
    AHEAD = 3
    TAIL = 16
    CH = UNIT // 2 * P
    WO_SLOTS = (17, 25)
    RING = 4

    LOAD_HEAD, K_HI, K_LO, Q_HI, Q_LO = -13, -9, -7, -8, -7

    def out_slot(o):
        return (o // QT + 1) * BT + 11 * (o % QT) // 8

    def mask_slot(n):
        return (n // QT - 1) * BT + 4 + 8 * (n % QT)

    def outs_of(r, t, shift=0):
        return [o for o in range(-OUTS if r is not FIRST else 0, OUTS)
                if out_slot(o) + shift == t]

    def masks_of(r, t, shift=0):
        return [n for n in range(QT, MASKS + QT if r is not LAST else MASKS) if mask_slot(n) + shift == t]

    def rounds(engine, slot):
        for t in range(-AHEAD, TILES):
            slot(FIRST, t)
        with engine.Fori(1, LAST) as r:
            for t in range(TILES):
                slot(r, t)
        for t in range(TILES + TAIL):
            slot(LAST, t)

    def two_banks(r, o):
        return r is LAST and o > OUTS - UNIT

    def head_at(r, t, step):
        h = (t - step) // QT
        return h if (t - step) % QT == 0 and not (r is FIRST and h < 1) and there(r, h, ALL_HEADS) else None

    def there(r, n, per):
        return not (r is FIRST and n < 0) and not (r is LAST and n >= per)

    with ExitStack() as ctx:
        def sb(name, shape, dt):
            return ctx.enter_context(nc.sbuf_tensor(name, shape, dt))

        def pb(name, shape, dt):
            return ctx.enter_context(nc.psum_tensor(name, shape, dt))

        def sem(name):
            return ctx.enter_context(nc.semaphore(name))

        wo_hi = sb("wo_hi", [P, 2, PAIRS, D], F32R)
        wo_lo = sb("wo_lo", [P, 2, PAIRS, D], F32R)
        bias_o = sb("bias_o", [P, D], F32)
        ident = sb("ident2", [P, P], F32)
        q_stack = sb("q_stack", [P, 2, N], F32R)
        k_hi = sb("k_hi", [P, 2, N], F32R)
        k_lo = sb("k_lo", [P, 2, N], F32R)
        q_raw = sb("q_raw", [P, N], F32)
        k_raw = sb("k_raw", [P, N], F32)
        v_pair = sb("v_pair", [P, 2, QT, P], F32)
        adj_in = sb("adj_in", [P, 2, N], I32)
        mask = sb("mask", [P, ROUND, QT, N], BF16)
        prob = sb("prob", [P, RING, N], F32)
        neg_max = sb("neg_max", [P, RING], F32)
        row_sum = sb("row_sum", [P, RING], F32)
        row_inv = sb("row_inv", [P, RING], F32)
        prob_t = sb("prob_t", [P, 2, QT, 2, CH], F32)
        att_hi = sb("att_hi", [P, PAIRS, 2, 2, CH], F32R)
        att_lo = sb("att_lo", [P, PAIRS, 2, 2, CH], F32R)
        x_res = sb("x_res", [P, 2, D], F32)
        z = sb("z", [P, RING, D], F32)
        wo_raw = z
        stats = sb("stats", [P, 6], F32)
        mean_var = sb("mean_var", [P, RING, 2], F32)
        half_power = sb("half_power", [P, 1], F32)
        var_eps = sb("var_eps", [P, 1], F32)
        neg_mean = sb("neg_mean", [P, 1], F32)
        inv_std = sb("inv_std", [P, 1], F32)

        score = [pb(f"score{n}", [P, N], F32) for n in range(2)]
        turned = [pb(f"turned{n}", [P, HALF], F32) for n in range(2)]
        mixed = pb("mixed", [P, HALF], F32)
        outp = pb("outp", [P, HALF], F32)

        wo_in = sem("wo_in")
        bias_in = sem("bias_o_in")
        wo_hi_done = sem("wo_hi_done")
        wo_lo_done = sem("wo_lo_done")
        ident_zero = sem("ident2_zero")
        ident_done = sem("ident2_done")
        k_in = sem("k_in")
        q_in = sem("q_in")
        k_hi_done = sem("k_hi_done")
        q_hi_done = sem("q_hi_done")
        k_split = sem("k_split")
        q_split = sem("q_split")
        v_in = [sem(f"v_in{n}") for n in range(2)]
        adj_in_done = [sem(f"adj_in_done{n}") for n in range(2)]
        x_in = [sem(f"x_in{n}") for n in range(2)]
        edges_made = sem("edges_made")
        masks_made = sem("masks_made")
        scored = sem("scored")
        masked = sem("masked")
        exped = sem("exped")
        inverted = sem("inverted")
        normed = sem("normed")
        transposed = sem("transposed")
        kept = [sem("kept_low"), sem("kept_high")]
        mixed_done = sem("mixed_done")
        att_hi_done = sem("att_hi_done")
        att_done = sem("att_done")
        projected = sem("projected")
        biased = sem("biased")
        summed = sem("summed")
        stat_done = sem("stat_done")
        ready = sem("ready")
        var_done = sem("var_done")
        std_done = sem("std_done")
        finished = sem("finished")
        z_free = [sem(f"z_free{n}") for n in range(RING)]

        def out_bank(r, o):
            return mixed if two_banks(r, o) and o % 2 == 1 else outp

        block = ctx.enter_context(nc.Block())

        def batch_rows(t, r, n):
            b = r * ROUND + n // QT
            where = slice(b, b + 1) if isinstance(b, int) else bass.ds(b, 1)
            q = n % QT
            return t[where, q * P:(q + 1) * P, :].rearrange("o p n -> p (o n)")

        @block.sync
        def _(sp):
            def load_wo(n):
                if n:
                    sp.wait_ge(wo_lo_done, n)
                for h in range(2):
                    sp.dma_start(wo_raw[h * HD:(h + 1) * HD, :, :],
                                 wo.rearrange("(g two p) n -> two p g n", two=2, p=HD)[(h + n) % 2, :, :, :]
                                 ).then_inc(wo_in, 16)


            def load_head(r, h):
                until(sp, k_split, r, ALL_HEADS, h)
                until(sp, q_split, r, ALL_HEADS, h)
                sp.nop(nofuse=True)
                b, rows = r * ROUND + h // HEADS, slice(h % HEADS * HD, (h % HEADS + 1) * HD)
                where = slice(b, b + 1) if isinstance(b, int) else bass.ds(b, 1)
                for dst, which, done in ((k_raw, 1, k_in), (q_raw, 0, q_in)):
                    for n in range(2):
                        sp.dma_start(dst[n * HD:(n + 1) * HD, :],
                                     qk_all[where, which, rows, :].rearrange("o p n -> p (o n)")).then_inc(done, 16)

            def load_v(r, pair):
                until(sp, mixed_done, r, UNITS, (pair - 1) * 4)
                sp.nop(nofuse=True)
                b, cols = r * ROUND + pair // PAIRS, slice(pair % PAIRS * P, (pair % PAIRS + 1) * P)
                where = slice(b, b + 1) if isinstance(b, int) else bass.ds(b, 1)
                sp.dma_start(v_pair[:, pair % 2, :, :],
                             v_all[where, :, cols].rearrange("o (t p) d -> p (o t) d", p=P)
                             ).then_inc(v_in[pair % 2], 16)

            def load_adj(r, n):
                until(sp, masks_made, r, MASKS, n - 1)
                sp.nop(nofuse=True)
                sp.dma_start(adj_in[:, n % 2, :], batch_rows(adj, r, n)).then_inc(adj_in_done[n % 2], 16)

            def load_x(r, o):
                until(sp, summed, r, OUTS, o - 1)
                sp.nop(nofuse=True)
                sp.dma_start(x_res[:, o % 2, :], batch_rows(x, r, o)).then_inc(x_in[o % 2], 16)

            def store(r, o):
                until(sp, finished, r, OUTS, o + 1)
                sp.nop(nofuse=True)
                sp.dma_start(batch_rows(out, r, o), z[:, o % RING, :]).then_inc(z_free[o % RING], 16)

            load_head(FIRST, 0)
            for n in range(2):
                load_adj(FIRST, n)
            load_head(FIRST, 1)
            for n in range(2, QT):
                load_adj(FIRST, n)
                if n == 3:
                    load_v(FIRST, 0)
            load_wo(0)

            def slot(r, t):
                h, pair = (t - LOAD_HEAD) // QT, (t - UNIT) // (2 * QT) + 1
                if r is FIRST and t == WO_SLOTS[1] - 4:
                    load_wo(1)
                    sp.dma_start(bias_o[:, :],
                                 bo.rearrange("(a n) -> a n", a=1).to_broadcast([P, D])).then_inc(bias_in, 16)
                if (t - LOAD_HEAD) % QT == 0 and h > 1 and there(r, h, ALL_HEADS):
                    load_head(r, h)
                if (t - UNIT) % (2 * QT) == 0 and there(r, pair, ALL_PAIRS):
                    load_v(r, pair)
                for n in masks_of(r, t, -3):
                    load_adj(r, n)
                for o in outs_of(r, t, -3):
                    load_x(r, o)
                for o in outs_of(r, t, 3):
                    store(r, o)

            rounds(sp, slot)
            for n in range(RING):
                sp.wait_ge(z_free[n], 16 + ROUNDS * OUTS // RING * 16)

        @block.gpsimd
        def _(pool):
            nc.gpsimd.memset(ident[:, :], 0.0).then_inc(ident_zero, 1)
            pool.wait_ge(ident_zero, 1)
            nc.gpsimd.affine_select(out=ident[:, :], in_=ident[:, :], compare_op=ALU.not_equal, fill=1.0,
                                    base=0, pattern=[[-1, P]], channel_multiplier=1).then_inc(ident_done, 1)
            nc.gpsimd.memset(half_power[:, :], -0.5).then_inc(ident_done, 1)


            def make_mask(r, n):
                until(pool, adj_in_done[n % 2], r, MASKS // 2 * 16, (n // 2 + 1) * 16)
                until(pool, masked, r, TILES, (n // QT - 1) * BT)
                pool.nop(nofuse=True)
                where = mask[:, n // QT % 2, n % QT, :]
                nc.gpsimd.tensor_scalar(where, adj_in[:, n % 2, :], 1.0, 0.0, ALU.min, ALU.max).then_inc(edges_made, 1)
                until(pool, edges_made, r, MASKS, n + 1 - QT)
                pool.nop(nofuse=True)
                nc.gpsimd.tensor_scalar(where, where, -MASKED, MASKED, ALU.mult, ALU.add).then_inc(masks_made, 1)

            def normalise(r, t):
                until(pool, inverted, r, TILES, t + 1)
                pool.nop(nofuse=True)
                nc.gpsimd.tensor_scalar(prob[:, t % RING, :], prob[:, t % RING, :],
                                        row_inv[:, t % RING:t % RING + 1], 1.0,
                                        ALU.mult, ALU.mult).then_inc(normed, 1)

            def k_low(r, h):
                until(pool, k_hi_done, r, ALL_HEADS, h + 1)
                nc.gpsimd.tensor_tensor(k_lo[:, h % 2, :], k_raw[:, :], k_hi[:, h % 2, :].bitcast(F32),
                                        ALU.subtract).then_inc(k_split, 1)

            def finish(r, o):
                until(pool, ready, r, OUTS, o + 1)
                until(pool, finished, r, OUTS, o)
                pool.nop(nofuse=True)
                nc.gpsimd.tensor_scalar(var_eps[:, :], mean_var[:, o % RING, 1:2], LN_EPS, None,
                                        ALU.add).then_inc(var_done, 1)
                nc.gpsimd.tensor_scalar(neg_mean[:, :], mean_var[:, o % RING, 0:1], -1.0, None,
                                        ALU.mult).then_inc(var_done, 1)
                until(pool, var_done, r, 2 * OUTS, 2 * (o + 1))
                nc.gpsimd.tensor_tensor(inv_std[:, :], var_eps[:, :], half_power[:, :], ALU.pow).then_inc(std_done, 1)
                until(pool, std_done, r, OUTS, o + 1)
                pool.nop(nofuse=True)
                nc.gpsimd.tensor_scalar(z[:, o % RING, :], z[:, o % RING, :], neg_mean[:, :], inv_std[:, :],
                                        ALU.add, ALU.mult).then_inc(finished, 1)

            pool.wait_ge(ident_done, 2)
            def slot(r, t):
                for o in outs_of(r, t, 1):
                    finish(r, o)
                if there(r, t + AHEAD - 1, TILES):
                    normalise(r, t + AHEAD - 1)
                if head_at(r, t, K_LO) is not None:
                    k_low(r, head_at(r, t, K_LO))
                for n in masks_of(r, t):
                    make_mask(r, n)

            rounds(pool, slot)

        @block.tensor
        def _(pe):
            pe.wait_ge(ident_done, 2)

            def scores(r, t):
                h, q = t // QT, t % QT
                buf = h % 2
                if q == 0:
                    until(pe, k_split, r, ALL_HEADS, h + 1)
                    until(pe, q_split, r, ALL_HEADS, h + 1)
                until(pe, masked, r, TILES, t - 1)
                for n, k in enumerate((k_hi, k_lo)):
                    for half in range(2):
                        cols = slice(half * HALF, (half + 1) * HALF)
                        last = nc.tensor.matmul(score[t % 2][:, cols], q_stack[:, buf, q * P:(q + 1) * P],
                                                k[:, buf, cols], start=n == 0, stop=n == 1)
                last.then_inc(scored, 1)

            def turn(r, t):
                until(pe, normed, r, TILES, t + 1)
                for half in range(2):
                    until(pe, kept[half], r, TILES, t)
                    for n in range(4):
                        k = half * 4 + n
                        last = nc.tensor.transpose(turned[half][:, n * P:(n + 1) * P],
                                                   prob[:, t % RING, k * P:(k + 1) * P], ident[:, :])
                    last.then_inc(transposed, 1)

            def mix(r, u, part):
                h = u * UNIT // QT
                pair = h // 2
                if part == 0:
                    if u % 4 == 0:
                        until(pe, v_in[pair % 2], r, ALL_PAIRS // 2 * 16, (pair // 2 + 1) * 16)
                    for half in range(2):
                        until(pe, kept[half], r, TILES, (u + 1) * UNIT)
                    until(pe, att_done, r, UNITS, u)
                for k in range(QT // PARTS * part, QT // PARTS * (part + 1)):
                    for n in range(2):
                        chunk = n if h % 2 == 0 else 1 - n
                        last = nc.tensor.matmul(mixed[n * HD:(n + 1) * HD, 0:CH],
                                                v_pair[:, pair % 2, k, h % 2 * HD:(h % 2 + 1) * HD],
                                                prob_t[:, u % 2, k, chunk, :], start=k == 0, stop=k == QT - 1)
                if part == PARTS - 1:
                    last.then_inc(mixed_done, 1)

            def project_out(r, o):
                q = o % QT
                of_head, chunk, off = q // 4, q % 4 // 2, q % 2 * P
                if r is FIRST and o == 0:
                    pe.wait_ge(wo_lo_done, 2)
                until(pe, att_done, r, UNITS, (o // QT + 1) * BU - 1 + of_head)
                until(pe, biased, r, OUTS, o - 1 if two_banks(r, o) else o)
                att, w = (att_hi, att_lo), (wo_hi, wo_lo)
                terms = [(a, c, g) for a, c in ((0, 0), (0, 1), (1, 0)) for g in range(PAIRS)]
                for n, (a, c, g) in enumerate(terms):
                    last = nc.tensor.matmul(out_bank(r, o)[:, :], att[a][:, g, of_head, chunk, off:off + P],
                                            w[c][:, chunk, g, :], start=n == 0, stop=n == len(terms) - 1)
                last.then_inc(projected, 1)

            def slot(r, t):
                u, step = t // UNIT - 1, UNIT // PARTS
                if there(r, t + AHEAD, TILES):
                    scores(r, t + AHEAD)
                if t % step == step - 1 and there(r, u, UNITS):
                    mix(r, u, t % UNIT // step)
                if t >= 0 and there(r, t, TILES):
                    turn(r, t)
                for o in outs_of(r, t):
                    project_out(r, o)

            rounds(pe, slot)

        def turned_out(half, t):
            in_unit = t % UNIT
            off = in_unit % 2 * P
            return prob_t[:, t // UNIT % 2, half * 4:half * 4 + 4, in_unit // 2, off:off + P]

        def att_part(att, u, n):
            h = u * UNIT // QT
            chunk = n if h % 2 == 0 else 1 - n
            return att[n * HD:(n + 1) * HD, h % HEADS // 2, u % 2, chunk, :]

        @block.scalar
        def _(act):
            def split_wo(n):
                act.wait_ge(wo_in, 32 * (n + 1))
                nc.scalar.activation(wo_hi[:, n, :, :], wo_raw[:, :, :], ACT.Copy).then_inc(wo_hi_done, 1)

            def head_hi(dst, raw, loaded, done, r, h):
                until(act, loaded, r, 32 * ALL_HEADS, 32 * (h + 1))
                until(act, scored, r, TILES, (h - 1) * QT)
                nc.scalar.activation(dst[:, h % 2, :], raw[:, :], ACT.Copy).then_inc(done, 1)

            def k_high(r, h):
                head_hi(k_hi, k_raw, k_in, k_hi_done, r, h)

            def q_high(r, h):
                head_hi(q_stack, q_raw, q_in, q_hi_done, r, h)

            def exponential(r, t):
                until(act, masked, r, TILES, t + 1)
                nc.scalar.activation(prob[:, t % RING, :], prob[:, t % RING, :], ACT.Exp,
                                     bias=neg_max[:, t % RING:t % RING + 1], scale=-1.0,
                                     accum_out=row_sum[:, t % RING:t % RING + 1]).then_inc(exped, 1)

            def keep_low(r, t):
                until(act, transposed, r, 2 * TILES, 2 * t + 1)
                if t % UNIT == 0:
                    until(act, mixed_done, r, UNITS, t // UNIT - 1)
                nc.scalar.activation(turned_out(0, t), turned[0][:, :].rearrange("p (k n) -> p k n", k=4),
                                     ACT.Copy).then_inc(kept[0], 1)

            def att_high(r, u):
                until(act, mixed_done, r, UNITS, u + 1)
                if u % BU < 2:
                    until(act, projected, r, OUTS, (u // BU - 1) * QT + (u % 2 + 1) * 4)
                for n in range(2):
                    nc.scalar.activation(att_part(att_hi, u, n), mixed[n * HD:(n + 1) * HD, 0:CH],
                                         ACT.Copy).then_inc(att_hi_done, 1)

            def slot(r, t):
                u = t // UNIT - 2
                if t % UNIT == 0 and there(r, u, UNITS):
                    att_high(r, u)
                if there(r, t + AHEAD - 1, TILES):
                    exponential(r, t + AHEAD - 1)
                if head_at(r, t, K_HI) is not None:
                    k_high(r, head_at(r, t, K_HI))
                if head_at(r, t, Q_HI) is not None:
                    q_high(r, head_at(r, t, Q_HI))
                if r is FIRST and t in WO_SLOTS:
                    split_wo(WO_SLOTS.index(t))
                if t >= 0 and there(r, t, TILES):
                    keep_low(r, t)

            k_high(FIRST, 0)
            q_high(FIRST, 0)
            rounds(act, slot)

        @block.vector
        def _(dve):
            def split_wo(n):
                dve.wait_ge(wo_hi_done, n + 1)
                nc.vector.tensor_tensor(wo_lo[:, n, :, :], wo_raw[:, :, :], wo_hi[:, n, :, :].bitcast(F32),
                                        ALU.subtract).then_inc(wo_lo_done, 1)

            def q_low(r, h):
                until(dve, q_hi_done, r, ALL_HEADS, h + 1)
                low = slice(HD, P)
                nc.vector.tensor_tensor(q_stack[low, h % 2, :], q_raw[low, :], q_stack[low, h % 2, :].bitcast(F32),
                                        ALU.subtract).then_inc(q_split, 1)

            def first_mask(n):
                dve.wait_ge(adj_in_done[n % 2], (n // 2 + 1) * 16)
                nc.vector.tensor_scalar(mask[:, 0, n, :], adj_in[:, n % 2, :], 0.0, MASKED,
                                        ALU.is_le, ALU.mult).then_inc(masks_made, 1)

            def mask_and_max(r, t):
                j, q = t // BT, t % QT
                if r is FIRST and t < QT:
                    first_mask(t)
                if t % BT < QT:
                    until(dve, masks_made, r, MASKS, j * QT + q + 1)
                until(dve, scored, r, TILES, t + 1)
                until(dve, transposed, r, 2 * TILES, 2 * (t - (RING - 1)))
                dve.nop(nofuse=True)
                nc.vector.tensor_tensor_reduce(out=prob[:, t % RING, :], in0=score[t % 2][:, :],
                                               in1=mask[:, j % 2, q, :], scale=-SCALE, scalar=3e38,
                                               op0=ALU.add, op1=ALU.min,
                                               accum_out=neg_max[:, t % RING:t % RING + 1]).then_inc(masked, 1)

            def invert(r, t):
                until(dve, exped, r, TILES, t + 1)
                nc.vector.reciprocal(row_inv[:, t % RING:t % RING + 1],
                                     row_sum[:, t % RING:t % RING + 1]).then_inc(inverted, 1)

            def keep_high(r, t):
                until(dve, transposed, r, 2 * TILES, 2 * t + 2)
                if t % UNIT == 0:
                    until(dve, mixed_done, r, UNITS, t // UNIT - 1)
                nc.vector.tensor_copy(turned_out(1, t), turned[1][:, :].rearrange("p (k n) -> p k n", k=4)
                                      ).then_inc(kept[1], 1)

            def att_low(r, u):
                until(dve, att_hi_done, r, 2 * UNITS, 2 * (u + 1))
                for n in range(2):
                    last = nc.vector.tensor_tensor(att_part(att_lo, u, n), mixed[n * HD:(n + 1) * HD, 0:CH],
                                                   att_part(att_hi, u, n).bitcast(F32), ALU.subtract)
                last.then_inc(att_done, 1)

            def add_norm(r, o):
                if r is FIRST and o == 0:
                    dve.wait_ge(bias_in, 16)
                until(dve, projected, r, OUTS, o + 1)
                until(dve, z_free[o % RING], r, OUTS // RING * 16, (o // RING + 1) * 16)
                nc.vector.tensor_tensor(z[:, o % RING, :], out_bank(r, o)[:, :], bias_o[:, :], ALU.add).then_inc(biased, 1)
                until(dve, biased, r, OUTS, o + 1)
                until(dve, x_in[o % 2], r, OUTS // 2 * 16, (o // 2 + 1) * 16)
                nc.vector.scalar_tensor_tensor(out=z[:, o % RING, :], in0=z[:, o % RING, :], scalar=0.0,
                                               in1=x_res[:, o % 2, :],
                                               op0=ALU.max, op1=ALU.add).then_inc(summed, 1)
                until(dve, summed, r, OUTS, o + 1)
                nc.vector.bn_stats(out=stats[:, :], in_=z[:, o % RING, :]).then_inc(stat_done, 1)
                until(dve, stat_done, r, OUTS, o + 1)
                dve.nop(nofuse=True)
                nc.vector.bn_aggr(out=mean_var[:, o % RING, :], in_=stats[:, :]).then_inc(ready, 1)

            for n in range(RING):
                dve.nop().then_inc(z_free[n], 16)

            def slot(r, t):
                u = t // UNIT - 2
                if t % UNIT == 0 and there(r, u, UNITS):
                    att_low(r, u)
                if there(r, t + AHEAD, TILES):
                    mask_and_max(r, t + AHEAD)
                if there(r, t + AHEAD - 1, TILES):
                    invert(r, t + AHEAD - 1)
                if head_at(r, t, Q_LO) is not None:
                    q_low(r, head_at(r, t, Q_LO))
                if r is FIRST and t - 2 in WO_SLOTS:
                    split_wo(WO_SLOTS.index(t - 2))
                if t >= 0 and there(r, t, TILES):
                    keep_high(r, t)
                for o in outs_of(r, t):
                    add_norm(r, o)

            dve.wait_ge(k_hi_done, 1)
            nc.vector.tensor_tensor(k_lo[:, 0, :], k_raw[:, :], k_hi[:, 0, :].bitcast(F32),
                                    ALU.subtract).then_inc(k_split, 1)
            q_low(FIRST, 0)
            rounds(dve, slot)


def build(nc, x, adj, wq, bq, wk, bk, wv, bv, wo, bo, out):
    qk_all = nc.dram_tensor("qk_all", (BATCH, 2, D, N), F32, kind="Internal").ap()
    v_all = nc.dram_tensor("v_all", (BATCH, N, D), F32, kind="Internal").ap()
    project(nc, x, wq, bq, wk, bk, wv, bv, qk_all, v_all)
    attend(nc, x, adj, wo, bo, qk_all, v_all, out)


_INS = ['x', 'adj', 'L0_gnn_Wq', 'L0_gnn_bq', 'L0_gnn_Wk', 'L0_gnn_bk', 'L0_gnn_Wv', 'L0_gnn_bv', 'L0_gnn_Wo',
        'L0_gnn_bo']


def kernel(**inputs):
    import numpy as _np
    import concourse.bacc as _bacc
    from concourse import mybir as _mybir
    from concourse.bass_utils import run_bass_kernel_spmd as _run

    nc = _bacc.Bacc("TRN2", target_bir_lowering=False, num_devices=1)
    arrays, args = {}, []
    for name in _INS:
        a = _np.ascontiguousarray(inputs[name])
        arrays[f"in_{name}_dram"] = a
        args.append(nc.dram_tensor(f"in_{name}_dram", a.shape, _mybir.dt.from_np(a.dtype), kind="ExternalInput").ap())
    out = nc.dram_tensor("out_0_dram", (BATCH, N, D), _mybir.dt.float32, kind="ExternalOutput").ap()
    build(nc, *args, out)
    r = _run(nc, [arrays], core_ids=[0])
    return r.results[0]["out_0_dram"]
```
